# Optimizing a Trainium2 kernel written in Bass

```python
import numpy as np
import jax
import jax.numpy as jnp

def _softmax(x, axis=-1):
    return jax.nn.softmax(x, axis=axis)

def _gelu(x):
    return jax.nn.gelu(x, approximate=True)

def _silu(x):
    return jax.nn.silu(x)

def _sigmoid(x):
    return jax.nn.sigmoid(x)

def _layernorm(x, axis=-1, eps=1e-05):
    m = jnp.mean(x, axis=axis, keepdims=True)
    v = jnp.var(x, axis=axis, keepdims=True)
    return (x - m) / jnp.sqrt(v + eps)

def _scatter_add(tgt, idx, src, axis=0):
    return tgt.at[idx].add(src)

def _segment_sum(src, seg, n):
    return jax.ops.segment_sum(src, seg, n)
kernel_name = 'mk_macaron_d1_jaxref_r8_fc11b5'

def setup_inputs(seed: int=0):
    np.random.seed(seed)
    _w = jnp.asarray

    def _L0_attn_setup():
        import math
        import jax, jax.numpy as jnp
        import numpy as np
        EMBED_DIM = 128
        NUM_HEADS = 16
        HEAD_DIM = EMBED_DIM // NUM_HEADS

        def _xavier(key, fan_in, fan_out):
            lim = math.sqrt(6.0 / (fan_in + fan_out))
            return jax.random.uniform(key, (fan_out, fan_in), jnp.float32, -lim, lim)
        key = jax.random.key(seed)
        kx, kq, kk, kv, ko = jax.random.split(key, 5)
        B, L = (4, 256)
        x = jax.random.normal(kx, (B, L, EMBED_DIM), jnp.float32)
        return {'x': x, 'wq': _xavier(kq, EMBED_DIM, EMBED_DIM), 'bq': jnp.zeros((EMBED_DIM,), jnp.float32), 'wk': _xavier(kk, EMBED_DIM, EMBED_DIM), 'bk': jnp.zeros((EMBED_DIM,), jnp.float32), 'wv': _xavier(kv, EMBED_DIM, EMBED_DIM), 'bv': jnp.zeros((EMBED_DIM,), jnp.float32), 'wo': _xavier(ko, EMBED_DIM, EMBED_DIM), 'bo': jnp.zeros((EMBED_DIM,), jnp.float32)}
    _L0_attn_in = _L0_attn_setup()

    def _L0_ffn_setup():
        import jax, jax.numpy as jnp
        import numpy as np
        EMB = 128
        FF = 4 * EMB

        def _ternary(w):
            scale = jnp.maximum(jnp.mean(jnp.abs(w)), 1e-08)
            w_t = jnp.clip(jnp.round(w / scale), -1.0, 1.0)
            return w + jax.lax.stop_gradient(w_t - w)
        key = jax.random.key(seed)
        kx, k1, k2, kb1, kb2 = jax.random.split(key, 5)
        x = jax.random.normal(kx, (4, 256, EMB), dtype=jnp.float32)
        lim1 = 1.0 / np.sqrt(EMB)
        lim2 = 1.0 / np.sqrt(FF)
        W1 = jax.random.uniform(k1, (FF, EMB), jnp.float32, -lim1, lim1)
        b1 = jax.random.uniform(kb1, (FF,), jnp.float32, -lim1, lim1)
        W2 = jax.random.uniform(k2, (EMB, FF), jnp.float32, -lim2, lim2)
        b2 = jax.random.uniform(kb2, (EMB,), jnp.float32, -lim2, lim2)
        return {'x': x, 'W1': W1, 'b1': b1, 'W2': W2, 'b2': b2}
    _L0_ffn_in = _L0_ffn_setup()
    _d = {'L0_attn_x': _L0_attn_in['x'], 'L0_attn_wq': _L0_attn_in['wq'], 'L0_attn_bq': _L0_attn_in['bq'], 'L0_attn_wk': _L0_attn_in['wk'], 'L0_attn_bk': _L0_attn_in['bk'], 'L0_attn_wv': _L0_attn_in['wv'], 'L0_attn_bv': _L0_attn_in['bv'], 'L0_attn_wo': _L0_attn_in['wo'], 'L0_attn_bo': _L0_attn_in['bo'], 'L0_ffn_W1': _L0_ffn_in['W1'], 'L0_ffn_b1': _L0_ffn_in['b1'], 'L0_ffn_W2': _L0_ffn_in['W2'], 'L0_ffn_b2': _L0_ffn_in['b2']}
    _x0 = _d['L0_attn_x']
    _d['L0_attn_x'] = jax.random.normal(jax.random.fold_in(jax.random.key(seed), 1), (16, 512, 128), dtype=_x0.dtype)
    del _x0
    return _d

def reference(L0_attn_x, L0_attn_wq, L0_attn_bq, L0_attn_wk, L0_attn_bk, L0_attn_wv, L0_attn_bv, L0_attn_wo, L0_attn_bo, L0_ffn_W1, L0_ffn_b1, L0_ffn_W2, L0_ffn_b2):

    def _L0_attn_ref(x, wq, bq, wk, bk, wv, bv, wo, bo):
        import math
        import jax, jax.numpy as jnp
        import numpy as np
        EMBED_DIM = 128
        NUM_HEADS = 16
        HEAD_DIM = EMBED_DIM // NUM_HEADS

        def _xavier(key, fan_in, fan_out):
            lim = math.sqrt(6.0 / (fan_in + fan_out))
            return jax.random.uniform(key, (fan_out, fan_in), jnp.float32, -lim, lim)
        B, L, D = x.shape
        H, Dh = (NUM_HEADS, HEAD_DIM)

        def proj(w, b):
            return (jnp.einsum('bld,ed->ble', x, w) + b).reshape(B, L, H, Dh).transpose(0, 2, 1, 3)
        q, k, v = (proj(wq, bq), proj(wk, bk), proj(wv, bv))
        scale = 1.0 / math.sqrt(H)
        scores = jnp.einsum('bhqd,bhkd->bhqk', q, k) * scale
        attn = jax.nn.softmax(scores, axis=-1)
        out = jnp.einsum('bhqk,bhkd->bhqd', attn, v)
        out = out.transpose(0, 2, 1, 3).reshape(B, L, D)
        return jnp.einsum('bld,ed->ble', out, wo) + bo

    def _L0_ffn_ref(x, W1, b1, W2, b2):
        import jax, jax.numpy as jnp
        import numpy as np
        EMB = 128
        FF = 4 * EMB

        def _ternary(w):
            scale = jnp.maximum(jnp.mean(jnp.abs(w)), 1e-08)
            w_t = jnp.clip(jnp.round(w / scale), -1.0, 1.0)
            return w + jax.lax.stop_gradient(w_t - w)
        h = jnp.einsum('bsd,fd->bsf', x, _ternary(W1)) + b1
        h = jax.nn.gelu(h, approximate=False)
        out = jnp.einsum('bsf,df->bsd', h, _ternary(W2)) + b2
        return out
    x = L0_attn_x
    x = x + 0.5 * _L0_ffn_ref(_layernorm(x, axis=-1), L0_ffn_W1, L0_ffn_b1, L0_ffn_W2, L0_ffn_b2)
    x = x + _L0_attn_ref(_layernorm(x, axis=-1), L0_attn_wq, L0_attn_bq, L0_attn_wk, L0_attn_bk, L0_attn_wv, L0_attn_bv, L0_attn_wo, L0_attn_bo)
    x = x + 0.5 * _L0_ffn_ref(_layernorm(x, axis=-1), L0_ffn_W1, L0_ffn_b1, L0_ffn_W2, L0_ffn_b2)
    return x

_drawn_inputs = setup_inputs


def setup_inputs(seed=0):
    import zlib

    import numpy as np

    out = dict(_drawn_inputs(seed))
    spreads = {'L0_attn_bq': (0.0, 0.8),
     'L0_attn_bk': (0.0, 2.0),
     'L0_attn_bv': (0.0, 0.8),
     'L0_attn_bo': (0.0, 2.0)}
    factors = {'L0_attn_wq': 8.0,
     'L0_attn_wk': 8.0,
     'L0_attn_wv': 8.0,
     'L0_attn_wo': 8.0,
     'L0_ffn_b1': 8.0,
     'L0_ffn_b2': 64.0}
    for name, (base, spread) in spreads.items():
        noise = np.random.default_rng([zlib.crc32(name.encode()), seed]).standard_normal(out[name].shape)
        drawn = base * np.exp(spread * noise) if base else spread * noise
        out[name] = jnp.asarray(drawn.astype(out[name].dtype))
    for name, factor in factors.items():
        out[name] = (out[name] * factor).astype(out[name].dtype)
    return out
```

```python
from contextlib import ExitStack

import concourse.bass as bass
from concourse import mybir

F32 = mybir.dt.float32
F32R = mybir.dt.float32r
ALU = mybir.AluOpType
ACT = mybir.ActivationFunctionType
AX = mybir.AxisListType

P = 128
EPS = 1e-5
HEADS = 16
GROUP = 4
HPG = GROUP // 2
BANK_OF = ((0, 1, 2, 1), (0, 2, 1, 2))
BANK_AGO = (4, 3, 3, 2)
ST_ORDER, S_ORDER = (0, 2, 1, 3), (1, 3, 0, 2)


def wait(engine, semaphore, value):
    if not isinstance(value, int) or value > 0:
        engine.wait_ge(semaphore, value)


def build(nc, x, w1, b1, w2, b2, wq, wk, wv, wo, bq, bk, bv, bo, out):
    B, L, D = x.shape
    F = w1.shape[1]
    TILES = L // P
    FT = F // P
    DH = D // HEADS
    NG = HEADS // GROUP
    STEPS = NG * TILES
    SCALE = 1.0 / HEADS ** 0.5
    VW = 32
    ROWS = 4 * DH
    MROW = ROWS

    with ExitStack() as ctx:
        def sb(name, shape, dt=F32):
            return ctx.enter_context(nc.sbuf_tensor(name, shape, dt))

        def sem(name):
            return ctx.enter_context(nc.semaphore(name))

        bank = [ctx.enter_context(nc.psum_tensor(f"bank{k}", [P, 512], F32)) for k in range(8)]
        s_bank, st_bank, o_bank, misc = bank[0:3], bank[3:6], bank[6], bank[7]
        f_h, f_t, f_o = bank[0:4], bank[4], bank[5]

        q_stack = nc.dram_tensor("q_stack", [B, HEADS, 4, DH, L], F32).ap()
        k_stack = nc.dram_tensor("k_stack", [B, HEADS, 4, DH, L], F32).ap()
        m_stack = nc.dram_tensor("m_stack", [B * NG, 2, 2 * HPG * TILES, P], F32).ap()

        res = sb("res", [P, B, TILES, D])
        w1_raw = sb("w1_raw", [P, F])
        w2_raw = sb("w2_raw", [P, F])
        w_abs = sb("w_abs", [P, 2, F])
        w_sum = sb("w_sum", [P, 2])
        w_scale = sb("w_scale", [P, 2])
        half_up, half_down = sb("half_up", [P, 2]), sb("half_down", [P, 2])
        w1_t = sb("w1_t", [P, F], F32R)
        w2_t = sb("w2_t", [P, FT, D])
        wq_s, wk_s, wv_s, wo_s = (sb(n, [P, D]) for n in ("wq_s", "wk_s", "wv_s", "wo_s"))
        b1_c = sb("b1_c", [P, FT])
        b2_r, b2_half, bv_r, bo_r = (sb(n, [P, D]) for n in ("b2_r", "b2_half", "bv_r", "bo_r"))
        bq_c, bq_scaled, bk_c = (sb(n, [P, 1]) for n in ("bq_c", "bq_scaled", "bk_c"))
        ones = sb("ones", [P, P])
        ident = sb("ident", [P, P])

        minus_half = sb("minus_half", [P, TILES])

        class Norm:

            def __init__(self, name, slots):
                self.slots = slots
                self.stats = sb(f"{name}_stats", [P, TILES, 6])
                self.mean_var = sb(f"{name}_mean_var", [P, slots, TILES, 2])
                self.var_eps = sb(f"{name}_var_eps", [P, slots, TILES])
                self.rstd = sb(f"{name}_rstd", [P, slots, TILES])
                self.shift = sb(f"{name}_shift", [P, slots, TILES])
                self.xn = sb(f"{name}_xn", [P, slots, TILES, D])

        ffn_norm, att_norm = Norm("ffn", 2), Norm("att", 1)
        x_hi = sb("x_hi", [P, 2, L], F32R)
        x_lo = sb("x_lo", [P, 2, L], F32R)
        h = sb("h", [P, 2, FT, L])

        x_t = sb("x_t", [P, L])
        q_full = sb("q_full", [P, L])
        k_full = sb("k_full", [P, L])
        q_parts = sb("q_parts", [P, 2, L], F32R)
        k_parts = sb("k_parts", [P, 2, L], F32R)
        v_aug = sb("v_aug", [P, 2, TILES, HEADS, VW])
        q_rows = sb("q_rows", [P, NG, HPG, L], F32R)
        k_rows = sb("k_rows", [P, NG, HPG, L], F32R)
        row_max = sb("row_max", [P, 2, 2, HPG, TILES])
        m_parts = sb("m_parts", [2 * HPG * TILES, 2, 2, P], F32R)
        probs = sb("probs", [P, 2, GROUP, L])
        o_sb = sb("o_sb", [P, 2, L])
        inv_sum = sb("inv_sum", [P, 2, TILES, GROUP])
        attn = sb("attn", [P, TILES, D])
        attn_t = sb("attn_t", [P, L])

        x_in = [sem("x_in_even"), sem("x_in_odd")]
        w_in, const_in = sem("w_in"), sem("const_in")
        w_step, w_ready, sums_ps, ident_set = sem("w_step"), sem("w_ready"), sem("sums_ps"), sem("ident_set")
        fixed_set = sem("fixed_set")

        class Ffn:

            def __init__(self, n):
                self.norm = ffn_norm
                self.stat_step = sem(f"f{n}_stat_step")
                self.rstd_ready = sem(f"f{n}_rstd_ready")
                self.norm_ready = sem(f"f{n}_norm_ready")
                self.xn_ready = sem(f"f{n}_xn_ready")
                self.t_ps = sem(f"f{n}_t_ps")
                self.hi_ready = sem(f"f{n}_hi_ready")
                self.lo_ready = sem(f"f{n}_lo_ready")
                self.h_ps = sem(f"f{n}_h_ps")
                self.h_ready = sem(f"f{n}_h_ready")
                self.o_ps = sem(f"f{n}_o_ps")
                self.biased = sem(f"f{n}_biased")
                self.done = sem(f"f{n}_done")

        ffn = [Ffn(0), Ffn(1)]

        xt_ps, xt_ready = sem("xt_ps"), sem("xt_ready")
        q_ps, k_ps, v_ps = sem("q_ps"), sem("k_ps"), sem("v_ps")
        q_ready, k_ready, v_ready = sem("q_ready"), sem("k_ready"), sem("v_ready")
        qh_ready, kh_ready, ql_ready, kl_ready = sem("qh_ready"), sem("kh_ready"), sem("ql_ready"), sem("kl_ready")
        stack_written = sem("stack_written")
        rows_in = [sem(f"rows_in{c}") for c in range(NG)]
        s_ps, s_used = sem("s_ps"), sem("s_used")
        mt_ps, mh_ready, ml_ready = sem("mt_ps"), sem("mh_ready"), sem("ml_ready")
        m_written = sem("m_written")
        m_in = [sem(f"m_in{c}") for c in range(NG)]
        st_ps, exp_done, pv_done = sem("st_ps"), sem("exp_done"), sem("pv_done")
        o_ready, ot_ps, inv_ready, attn_ready = sem("o_ready"), sem("ot_ps"), sem("inv_ready"), sem("attn_ready")
        at_ps, at_ready, op_ps = sem("at_ps"), sem("at_ready"), sem("op_ps")
        att_biased, att_done = sem("att_biased"), sem("att_done")
        stored = sem("stored")

        class Att:

            norm = att_norm
            stat_step, rstd_ready = sem("stat_step"), sem("rstd_ready")
            norm_ready, xn_ready = sem("norm_ready"), sem("xn_ready")

        att = Att

        def ln_stats(e, t, before, s):
            before()
            for j in range(TILES):
                i = e.bn_stats(s.norm.stats[:, j, :], res[:, t, j, :])
            i.then_inc(s.stat_step, 1)

        def ln_stats_done(e, t, s):
            wait(e, s.xn_ready, t + 1 - s.norm.slots)
            e.wait_ge(s.stat_step, 3 * t + 1)

        def ln_aggregate(e, t, slot, s):
            if isinstance(t, int):
                ln_stats_done(e, t, s)
            for j in range(TILES):
                i = e.bn_aggr(s.norm.mean_var[:, slot, j, :], s.norm.stats[:, j, :])
            i.then_inc(s.stat_step, 1)

        def ln_add_eps(e, t, slot, s):
            e.wait_ge(s.stat_step, 3 * t + 2)
            e.tensor_scalar(s.norm.var_eps[:, slot, :], s.norm.mean_var[:, slot, :, 1], EPS, None, ALU.add)\
                .then_inc(s.stat_step, 1)

        def ln_rstd(e, t, slot, s):
            e.wait_ge(s.stat_step, 3 * t + 3)
            e.tensor_tensor(s.norm.rstd[:, slot, :], s.norm.var_eps[:, slot, :], minus_half[:, :], ALU.pow)\
                .then_inc(s.rstd_ready, 1)

        def ln_shift(e, t, slot, s):
            e.wait_ge(s.rstd_ready, t + 1)
            e.scalar_tensor_tensor(s.norm.shift[:, slot, :], s.norm.mean_var[:, slot, :, 0], -1.0,
                                   s.norm.rstd[:, slot, :], ALU.mult, ALU.mult).then_inc(s.norm_ready, 1)

        def normalise(e, t, slot, s, used, tiles=range(TILES)):
            if tiles[0] == 0:
                e.wait_ge(s.norm_ready, t + 1)
                wait(e, used[0], used[1])
            for j in tiles:
                i = e.activation(s.norm.xn[:, slot, j, :], res[:, t, j, :], ACT.Identity,
                                 bias=s.norm.shift[:, slot, j:j + 1], scale=s.norm.rstd[:, slot, j:j + 1])
            if tiles[-1] == TILES - 1:
                i.then_inc(s.xn_ready, 1)

        def parts_of(t):
            if not isinstance(t, int):
                return True, True, True, True, True
            return t < B, 1 <= t <= B, t >= 2, t + 1 < B, t + 2 < B

        def ffn_middle(e, step):
            step(2, 0)
            step(3, 1)
            with e.Fori(4, B - 4, 2) as t:
                step(t, 0)
                step(t + 1, 1)

        def ffn_end(e, step):
            for t in range(B - 4, B + 2):
                step(t, t % 2)

        def ffn_tensor(e, s):
            def step(t, slot, between=None):
                transpose, hidden, output, _, _ = parts_of(t)
                if transpose:
                    e.wait_ge(s.xn_ready, t + 1)
                    wait(e, s.lo_ready, t)
                    for j in range(TILES):
                        i = e.transpose(f_t[:, j * P:(j + 1) * P], s.norm.xn[:, slot, j, :], ident[:, :])
                    i.then_inc(s.t_ps, 1)
                if hidden:
                    e.wait_ge(s.lo_ready, t)
                    for f in range(FT):
                        wait(e, s.h_ready, (t - 2) * FT + f + 1)
                        e.matmul(f_h[f][:, :], w1_t[:, f * P:(f + 1) * P], x_hi[:, 1 - slot, :],
                                 start=True, stop=False)
                        e.matmul(f_h[f][:, :], w1_t[:, f * P:(f + 1) * P], x_lo[:, 1 - slot, :],
                                 start=False, stop=True).then_inc(s.h_ps, 1)
                if output:
                    e.wait_ge(s.h_ready, (t - 1) * FT)
                    wait(e, s.done, t - 2)
                    for j in range(TILES):
                        if between:
                            between(j)
                        for f in range(FT):
                            i = e.matmul(f_o[:, j * D:(j + 1) * D], h[:, slot, f, j * P:(j + 1) * P],
                                         w2_t[:, f, :], start=(f == 0), stop=(f == FT - 1))
                    i.then_inc(s.o_ps, 1)
            return step

        def ffn_scalar(e, s):
            def step(t, slot):
                transpose, hidden, _, norm, _ = parts_of(t)
                if transpose:
                    e.wait_ge(s.t_ps, t + 1)
                    wait(e, s.h_ps, (t - 1) * FT)
                    e.activation(x_hi[:, slot, :], f_t[:, :], ACT.Copy).then_inc(s.hi_ready, 1)
                if norm:
                    normalise(e, t + 1, 1 - slot, s, (s.t_ps, t))
                if hidden:
                    wait(e, s.o_ps, t - 2)
                    for f in range(FT):
                        e.wait_ge(s.h_ps, (t - 1) * FT + f + 1)
                        e.activation(h[:, 1 - slot, f, :], f_h[f][:, :], ACT.Gelu, bias=b1_c[:, f:f + 1])\
                            .then_inc(s.h_ready, 1)
            return step

        def ffn_vector(e, s, before):
            def first_norm(t):
                ln_stats(e, t, lambda: before(t, t), s)
                ln_aggregate(e, t, t, s)
                ln_add_eps(e, t, t, s)
                ln_shift(e, t, t, s)

            def step(t, slot):
                transpose, _, output, _, stats = parts_of(t)
                if stats:
                    ln_stats(e, t + 2, lambda: before(t + 2, slot), s)
                    if not isinstance(t, int):
                        ln_stats_done(e, t + 2, s)
                if transpose:
                    e.wait_ge(s.hi_ready, t + 1)
                    wait(e, s.h_ps, (t - 1) * FT)
                    e.tensor_tensor(x_lo[:, slot, :], f_t[:, :], x_hi[:, slot, :], ALU.subtract)\
                        .then_inc(s.lo_ready, 1)
                if stats:
                    ln_aggregate(e, t + 2, slot, s)
                    ln_add_eps(e, t + 2, slot, s)
                    ln_shift(e, t + 2, slot, s)
                if output:
                    e.wait_ge(s.o_ps, t - 1)
                    e.wait_ge(s.biased, t - 1)
                    r = res[:, t - 2, :, :].rearrange("p j d -> p (j d)")
                    e.scalar_tensor_tensor(r, f_o[:, :], 0.5, r, ALU.mult, ALU.add).then_inc(s.done, 1)
            return step, first_norm

        def add_row(e, t, row, xn_done, signal):
            e.wait_ge(xn_done, t + 1)
            e.tensor_tensor(res[:, t, :, :], res[:, t, :, :],
                            row[:, :].unsqueeze(1).broadcast_to([P, TILES, D]), ALU.add).then_inc(signal, 1)

        def ffn_gpsimd(e, s):
            def step(t, slot):
                if parts_of(t)[-1]:
                    ln_rstd(e, t + 2, slot, s)
                add_row(e, t, b2_half, s.xn_ready, s.biased)
            return step

        V_STEP, AT_STEP, OP_STEP, X_STEP, Q_STEP, K_STEP = 2, 3, 6, 10, 11, 14
        NORM_AT = ((X_STEP - 1, 1), (X_STEP - 1, 3), (X_STEP, 1))

        def attention_batches(e, batch):
            batch(0, 0)
            with e.Fori(1, B - 3, 2) as b:
                batch(b, 1)
                batch(b + 1, 0)
            for b in range(B - 3, B):
                batch(b, b % 2)

        def neighbours(b):
            if not isinstance(b, int):
                return True, True, True
            return b > 0, b + 1 < B, b + 2 < B

        def att_tensor(e):
            def half(i):
                return 64 * (i % 2), i // 2

            def transposed_x(b):
                e.wait_ge(att.xn_ready, b + 1)
                for j in range(TILES):
                    m = e.transpose(misc[:, j * P:(j + 1) * P], att_norm.xn[:, 0, j, :], ident[:, :])
                m.then_inc(xt_ps, 1)

            def project_q(b):
                e.wait_ge(xt_ready, b + 1)
                e.matmul(misc[:, :], wq_s[:, :], x_t[:, :], start=True, stop=True).then_inc(q_ps, 1)

            def project_k(b):
                e.matmul(misc[:, :], wk_s[:, :], x_t[:, :], start=True, stop=True).then_inc(k_ps, 1)

            def project_v(b):
                for j in range(TILES):
                    m = e.matmul(misc[:, j * D:(j + 1) * D], x_t[:, j * P:(j + 1) * P], wv_s[:, :],
                                 start=True, stop=True)
                m.then_inc(v_ps, 1)

            def score(g, c, kt, i):
                n = 16 * g + 4 * kt + i
                if i > 0:
                    wait(e, s_used, n + 1 - BANK_AGO[i])
                p, hh = half(S_ORDER[i])
                e.matmul(s_bank[BANK_OF[kt % 2][i]][:, :], q_rows[p:p + 64, c, hh, kt * P:(kt + 1) * P],
                         k_rows[p:p + 64, c, hh, :], start=True, stop=True).then_inc(s_ps, 1)

            def shifted(g, c, kt, i):
                n = 16 * g + 4 * kt + i
                if i in (1, 3):
                    wait(e, exp_done, n + 1 - BANK_AGO[i])
                p, hh = half(ST_ORDER[i])
                e.matmul(st_bank[BANK_OF[kt % 2][i]][:, :], k_rows[p:p + 64, c, hh, kt * P:(kt + 1) * P],
                         q_rows[p:p + 64, c, hh, :], start=True, stop=True).then_inc(st_ps, 1)

            def weighted(g, c, kt, vslot):
                if kt == 0:
                    wait(e, o_ready, g)
                e.wait_ge(exp_done, 16 * g + 4 * kt + 4)
                for i in range(GROUP):
                    m = e.matmul(o_bank[VW * i:VW * i + VW, :], v_aug[:, vslot, kt, GROUP * c + i, :],
                                 probs[:, kt % 2, i, :], start=(kt == 0), stop=(kt == TILES - 1))
                m.then_inc(pv_done, 1)

            def transposed_max(g, slot):
                e.wait_ge(s_used, 16 * g + 16)
                e.transpose(misc[0:4 * TILES, 0:P],
                            row_max[:, slot, :, :, :].rearrange("p a b j -> p (a b j)"), ident[:, :])\
                    .then_inc(mt_ps, 1)

            def transposed_o(g, slot):
                e.wait_ge(o_ready, g + 1)
                for j in range(TILES):
                    m = e.transpose(misc[:, j * P:(j + 1) * P], o_sb[:, slot, j * P:(j + 1) * P], ident[:, :])
                m.then_inc(ot_ps, 1)

            def transposed_attn(b):
                e.wait_ge(attn_ready, NG * b + NG)
                for j in range(TILES):
                    m = e.transpose(misc[:, j * P:(j + 1) * P], attn[:, j, :], ident[:, :])
                m.then_inc(at_ps, 1)

            def project_out(b):
                e.wait_ge(at_ready, b + 1)
                for j in range(TILES):
                    m = e.matmul(misc[:, j * D:(j + 1) * D], attn_t[:, j * P:(j + 1) * P], wo_s[:, :],
                                 start=True, stop=True)
                m.then_inc(op_ps, 1)

            def small_work(b, s):
                before, after, after2 = neighbours(b)
                c, kt = s // TILES, s % TILES
                g = NG * b + c
                if kt == 0 and (c + 1 < NG or after):
                    if s == 0:
                        if after:
                            e.wait_ge(k_ready, b + 2)
                        else:
                            e.wait_ge(attn_ready, NG * b - 1)
                    elif s == 4:
                        if before:
                            e.wait_ge(at_ready, b)
                        else:
                            e.wait_ge(v_ready, b + 2)
                    elif s == 8:
                        if before:
                            e.wait_ge(att_done, b)
                        else:
                            e.wait_ge(attn_ready, NG * b + 1)
                    elif after2:
                        e.wait_ge(q_ready, b + 3)
                    else:
                        e.wait_ge(attn_ready, NG * b + 2)
                    e.wait_ge(ml_ready, g + 1)
                    transposed_max(g + 1, (c + 1) % 2)
                elif kt == 1 and (c > 0 or before):
                    if c + 1 < NG or after:
                        e.wait_ge(ml_ready, g + 2)
                    else:
                        e.wait_ge(attn_ready, g - 1)
                    transposed_o(g - 1, (c - 1) % 2)
                elif s == V_STEP and after:
                    if before:
                        e.wait_ge(attn_ready, NG * b)
                    else:
                        e.wait_ge(ml_ready, g + 2)
                    project_v(b + 1)
                elif s == AT_STEP and before:
                    if after:
                        e.wait_ge(v_ready, b + 2)
                    transposed_attn(b - 1)
                elif s == OP_STEP and before:
                    e.wait_ge(attn_ready, NG * b + 1)
                    project_out(b - 1)
                elif s == X_STEP and after2:
                    e.wait_ge(attn_ready, NG * b + 2)
                    transposed_x(b + 2)
                elif s == Q_STEP and after2:
                    project_q(b + 2)
                elif s == K_STEP and after2:
                    e.wait_ge(attn_ready, NG * b + 3)
                    project_k(b + 2)

            def batch(b, slot):
                before, after, _ = neighbours(b)
                for s in range(STEPS):
                    c, kt = s // TILES, s % TILES
                    g = NG * b + c
                    ahead = c + 2 < NG or after
                    cs = (c + 2) % NG
                    if kt == 0:
                        e.wait_ge(m_in[c], 32 * (b + 1))
                        if ahead:
                            e.wait_ge(rows_in[cs], 96 * (b + 1 + (c + 2) // NG))
                    for i in range(GROUP):
                        shifted(g, c, kt, i)
                        if ahead:
                            score(g + 2, cs, kt, i)
                        if i == 1:
                            if s > 0:
                                weighted(NG * b + (s - 1) // TILES, (s - 1) // TILES, (s - 1) % TILES, slot)
                            elif before:
                                weighted(g - 1, NG - 1, TILES - 1, 1 - slot)
                    small_work(b, s)

            def before_step(t):
                if t == B - 2:
                    project_q(0)
                elif t == B - 1:
                    e.wait_ge(k_ready, 1)
                    project_v(0)
                elif t == B:
                    project_q(1)

            def after_step(t):
                if t == B - 3:
                    transposed_x(0)
                elif t == B - 2:
                    e.wait_ge(q_ready, 1)
                    project_k(0)
                elif t == B - 1:
                    e.wait_ge(v_ready, 1)
                    transposed_x(1)
                elif t == B:
                    e.wait_ge(q_ready, 2)
                    project_k(1)

            def first_scores(j):
                if j == 0:
                    e.wait_ge(rows_in[0], 96)
                    e.wait_ge(ffn[0].h_ready, B * FT)
                for i in range(GROUP):
                    score(0, 0, j, i)

            def begin(step):
                for t in range(B - 4, B + 1):
                    before_step(t)
                    step(t, t % 2)
                    after_step(t)
                step(B + 1, 1, first_scores)
                e.wait_ge(k_ready, 2)
                transposed_max(0, 0)
                e.wait_ge(rows_in[1], 96)
                for kt in range(TILES):
                    for i in range(GROUP):
                        score(1, 1, kt, i)
                e.wait_ge(ffn[0].done, B)
                attention_batches(e, batch)

            last = NG * B - 1

            def end(step):
                weighted(last, NG - 1, TILES - 1, 1)
                e.wait_ge(exp_done, 16 * (last + 1))
                step(0, 0)
                e.wait_ge(attn_ready, last)
                transposed_o(last, 1)
                step(1, 1)
                transposed_attn(B - 1)
                step(2, 0)
                project_out(B - 1)
                step(3, 1)
            return begin, end

        def att_scalar(e):
            def x_transposed(b):
                e.wait_ge(xt_ps, b + 1)
                wait(e, v_ps, b)
                e.activation(x_t[:, :], misc[:, :], ACT.Copy).then_inc(xt_ready, 1)

            def q_out(b):
                e.wait_ge(q_ps, b + 1)
                wait(e, ql_ready, b)
                e.activation(q_full[:, :], misc[:, :], ACT.Identity, bias=bq_scaled[:, :], scale=SCALE)\
                    .then_inc(q_ready, 1)

            def k_out(b):
                e.wait_ge(k_ps, b + 1)
                wait(e, kl_ready, b)
                e.activation(k_full[:, :], misc[:, :], ACT.Identity, bias=bk_c[:, :]).then_inc(k_ready, 1)

            def max_high(g, slot):
                e.wait_ge(mt_ps, g + 1)
                wait(e, m_written, 16 * (g - 1))
                e.activation(m_parts[:, slot, 0, :], misc[0:4 * TILES, 0:P], ACT.Copy, scale=-1.0)\
                    .then_inc(mh_ready, 1)

            def o_out(g, slot):
                e.wait_ge(pv_done, TILES * (g + 1))
                wait(e, ot_ps, g - 1)
                e.activation(o_sb[:, slot, :], o_bank[:, :], ACT.Copy).then_inc(o_ready, 1)

            def attn_out(b):
                e.wait_ge(at_ps, b + 1)
                wait(e, op_ps, b)
                e.activation(attn_t[:, :], misc[:, :], ACT.Copy).then_inc(at_ready, 1)

            def batch(b, slot):
                before, after, after2 = neighbours(b)
                for s in range(STEPS):
                    c, kt = s // TILES, s % TILES
                    g = NG * b + c
                    wait(e, pv_done, STEPS * b + s - 1)
                    for i in range(GROUP):
                        n = 16 * g + 4 * kt + i
                        e.wait_ge(st_ps, n + 1)
                        e.activation(probs[:, kt % 2, ST_ORDER[i], :], st_bank[BANK_OF[kt % 2][i]][:, :], ACT.Exp)\
                            .then_inc(exp_done, 1)
                        if kt == 0 and i == 2 and (c > 0 or before):
                            o_out(g - 1, (c - 1) % 2)
                        if after2 and (s, i) in NORM_AT:
                            j = 1 + NORM_AT.index((s, i))
                            normalise(e, b + 2, 0, att, (xt_ps, b + 2), range(j, j + 1))
                    if kt == 0:
                        if c + 1 < NG or after:
                            max_high(g + 1, (c + 1) % 2)
                    if s == AT_STEP and before:
                        attn_out(b - 1)
                    if after2:
                        if s == X_STEP - 2:
                            normalise(e, b + 2, 0, att, (xt_ps, b + 2), range(0, 1))
                        elif s == X_STEP:
                            x_transposed(b + 2)
                        elif s == Q_STEP:
                            q_out(b + 2)
                        elif s == K_STEP:
                            k_out(b + 2)

            def begin(step):
                for t in range(B - 4, B + 1):
                    step(t, t % 2)
                    if t == B - 4:
                        normalise(e, 0, 0, att, (xt_ps, 0))
                    elif t == B - 3:
                        x_transposed(0)
                        normalise(e, 1, 0, att, (xt_ps, 1))
                    elif t == B - 2:
                        q_out(0)
                        k_out(0)
                    elif t == B - 1:
                        x_transposed(1)
                    else:
                        q_out(1)
                        k_out(1)
                max_high(0, 0)
                attention_batches(e, batch)

            def end(step, first_norm):
                first_norm()
                o_out(NG * B - 1, 1)
                step(0, 0)
                step(1, 1)
                attn_out(B - 1)
                step(2, 0)
                step(3, 1)
            return begin, end

        def att_vector(e):
            def split(full, parts, source, signal, b):
                e.wait_ge(source, b + 1)
                wait(e, stack_written, 128 * b)
                e.tensor_copy(parts[:, 0, :], full[:, :]).then_inc(signal, 1)

            def v_out(b, slot):
                e.wait_ge(v_ps, b + 1)
                wait(e, pv_done, STEPS * (b - 1))
                e.tensor_tensor(v_aug[:, slot, :, :, 0:DH],
                                misc[:, :].rearrange("p (j h d) -> p j h d", j=TILES, d=DH),
                                bv_r[:, :].rearrange("p (h d) -> p h d", d=DH).unsqueeze(1)
                                .broadcast_to([P, TILES, HEADS, DH]), ALU.add).then_inc(v_ready, 1)

            def reduce_scores(g, c, kt, i, slot):
                n = 16 * g + 4 * kt + i
                if kt == 0 and i == 0:
                    wait(e, mt_ps, g - 1)
                e.wait_ge(s_ps, n + 1)
                head = S_ORDER[i]
                e.tensor_reduce(row_max[:, slot, head % 2, head // 2, kt:kt + 1], s_bank[BANK_OF[kt % 2][i]][:, :],
                                AX.X, ALU.max).then_inc(s_used, 1)

            def max_low(g, slot):
                e.wait_ge(mh_ready, g + 1)
                e.scalar_tensor_tensor(m_parts[:, slot, 1, :], misc[0:4 * TILES, 0:P], -1.0,
                                       m_parts[:, slot, 0, :], ALU.mult, ALU.subtract).then_inc(ml_ready, 1)

            o_view = misc[:, :].rearrange("p (j i r) -> p j i r", j=TILES, r=VW)

            def o_sums(g, slot):
                e.wait_ge(ot_ps, g + 1)
                e.reciprocal(inv_sum[:, slot, :, :], o_view[:, :, :, DH]).then_inc(inv_ready, 1)

            def o_scaled(b, g, c, slot):
                if c == 0:
                    wait(e, at_ps, b)
                e.wait_ge(inv_ready, g + 1)
                e.tensor_tensor(attn[:, :, GROUP * DH * c:GROUP * DH * (c + 1)].rearrange("p j (i d) -> p j i d", d=DH),
                                o_view[:, :, :, 0:DH],
                                inv_sum[:, slot, :, :].unsqueeze(3).broadcast_to([P, TILES, GROUP, DH]),
                                ALU.mult).then_inc(attn_ready, 1)

            def residual(b):
                e.wait_ge(op_ps, b + 1)
                e.wait_ge(att_biased, b + 1)
                r = res[:, b, :, :].rearrange("p j d -> p (j d)")
                e.tensor_tensor(r, misc[:, :], r, ALU.add).then_inc(att_done, 1)

            def batch(b, slot, hook=None):
                before, after, after2 = neighbours(b)
                for s in range(STEPS):
                    c, kt = s // TILES, s % TILES
                    g = NG * b + c
                    ahead = c + 2 < NG or after
                    cs = (c + 2) % NG
                    for i in range(GROUP):
                        if s == 6 and i == 1 and after2 and not isinstance(b, int):
                            ln_stats_done(e, b + 2, att)
                        if ahead:
                            reduce_scores(g + 2, cs, kt, i, c % 2)
                        if kt == 1 and i == 0 and (c + 1 < NG or after):
                            max_low(g + 1, (c + 1) % 2)
                        if kt == 1 and i == 3 and (c > 0 or before):
                            o_sums(g - 1, (c - 1) % 2)
                        if kt == 2 and i == 0 and (c > 0 or before):
                            o_scaled(b, g - 1, (c - 1) % NG, (c - 1) % 2)
                        if s == V_STEP + 1 and i == 0 and after:
                            v_out(b + 1, 1 - slot)
                        if s == OP_STEP + 1 and i == 0 and before:
                            residual(b - 1)
                        if after2:
                            if s == 5 and i == 1:
                                ln_stats(e, b + 2, lambda: e.wait_ge(ffn[0].done, b + 3), att)
                            elif s == 6 and i == 1:
                                ln_aggregate(e, b + 2, 0, att)
                            elif s == 6 and i == 3:
                                ln_add_eps(e, b + 2, 0, att)
                            elif s == 8 and i == 0:
                                ln_shift(e, b + 2, 0, att)
                            elif s == Q_STEP + 1 and i == 0:
                                split(q_full, q_parts, q_ready, qh_ready, b + 2)
                            elif s == K_STEP + 1 and i == 0:
                                split(k_full, k_parts, k_ready, kh_ready, b + 2)

            def norm(b):
                ln_stats(e, b, lambda: e.wait_ge(ffn[0].done, b + 1), att)
                ln_aggregate(e, b, 0, att)
                ln_add_eps(e, b, 0, att)
                ln_shift(e, b, 0, att)

            def begin(step):
                for t in range(B - 4, B + 1):
                    step(t, t % 2)
                    if t == B - 4:
                        norm(0)
                    elif t == B - 3:
                        norm(1)
                    elif t == B - 2:
                        split(q_full, q_parts, q_ready, qh_ready, 0)
                        split(k_full, k_parts, k_ready, kh_ready, 0)
                    elif t == B - 1:
                        e.wait_ge(fixed_set, 7)
                        v_out(0, 0)
                    else:
                        split(q_full, q_parts, q_ready, qh_ready, 1)
                for kt in range(TILES):
                    for i in range(GROUP):
                        reduce_scores(0, 0, kt, i, 0)
                    if kt == 0:
                        split(k_full, k_parts, k_ready, kh_ready, 1)
                step(B + 1, 1)
                for kt in range(TILES):
                    for i in range(GROUP):
                        reduce_scores(1, 1, kt, i, 1)
                        if kt == 0 and i == 2:
                            max_low(0, 0)
                attention_batches(e, batch)

            def end(step, first_norm):
                first_norm(0)
                first_norm(1)
                step(0, 0)
                o_sums(NG * B - 1, 1)
                o_scaled(B, NG * B - 1, NG - 1, 1)
                step(1, 1)
                step(2, 0)
                residual(B - 1)
                step(3, 1)
            return begin, end

        def att_gpsimd(e):
            def low(full, parts, high_ready, signal, b):
                e.wait_ge(high_ready, b + 1)
                e.tensor_tensor(parts[:, 1, :], full[:, :], parts[:, 0, :], ALU.subtract).then_inc(signal, 1)

            def batch(b):
                low(q_full, q_parts, qh_ready, ql_ready, b)
                low(k_full, k_parts, kh_ready, kl_ready, b)
                add_row(e, b, bo_r, att.xn_ready, att_biased)

            def begin(step):
                for t in range(B - 4, B):
                    step(t, t % 2)
                    if t == B - 4:
                        ln_rstd(e, 0, 0, att)
                    elif t == B - 3:
                        ln_rstd(e, 1, 0, att)
                    elif t == B - 2:
                        batch(0)
                batch(1)
                ln_rstd(e, 2, 0, att)
                with e.Fori(2, B - 1) as b:
                    batch(b)
                    ln_rstd(e, b + 1, 0, att)
                batch(B - 1)
            return begin

        def att_sync(e):
            def store_parts(b):
                for ready, parts, stack, order in ((ql_ready, q_parts, q_stack, (0, 1, 0, 1)),
                                                   (kl_ready, k_parts, k_stack, (0, 1, 1, 0))):
                    e.wait_ge(ready, b + 1)
                    for r, part in enumerate(order):
                        e.dma_start(stack[b, :, r, :, :], parts[:, part, :].bitcast(F32)).then_inc(stack_written, 16)

            def load_rows(b, c):
                wait(e, st_ps, 16 * (NG * b + c - NG + 1))
                for half in range(2):
                    e.dma_start(q_rows[64 * half + MROW:64 * half + MROW + 2, c, :, :].bitcast(F32),
                                q_rows[64 * half + MROW + 2:64 * half + MROW + 4, c, :, :].bitcast(F32))\
                        .then_inc(rows_in[c], 16)
                if c == 0:
                    e.wait_ge(stack_written, 128 * (b + 1))
                for half in range(2):
                    for rows, stack in ((q_rows, q_stack), (k_rows, k_stack)):
                        heads = stack[b, GROUP * c + half:GROUP * (c + 1):2, :, :, :]
                        e.dma_start(rows[64 * half:64 * half + ROWS, c, :, :].bitcast(F32),
                                    heads.rearrange("a r d n -> (r d) a n")).then_inc(rows_in[c], 16)

            def load_max(b, c, slot):
                g = NG * b + c
                e.wait_ge(ml_ready, g + 1)
                e.dma_start(m_stack[g].rearrange("t r p -> r t p"), m_parts[:, slot, :, :].bitcast(F32))\
                    .then_inc(m_written, 16)
                e.wait_ge(m_written, 16 * (g + 1))
                for half in range(2):
                    e.dma_start(q_rows[64 * half + MROW:64 * half + MROW + 2, c, :, :].bitcast(F32),
                                m_stack[g, :, HPG * TILES * half:HPG * TILES * (half + 1), :]
                                .rearrange("t (a j) p -> t a (j p)", a=HPG)).then_inc(m_in[c], 16)

            def batch(b, slot):
                _, after, after2 = neighbours(b)
                for c in range(NG):
                    if c + 3 < NG or after:
                        load_rows(b + (c + 3) // NG, (c + 3) % NG)
                    if c + 1 < NG or after:
                        load_max(b + (c + 1) // NG, (c + 1) % NG, (c + 1) % 2)
                if after2:
                    store_parts(b + 2)

            e.wait_ge(fixed_set, 7)
            store_parts(0)
            for c in range(3):
                load_rows(0, c)
            store_parts(1)
            load_max(0, 0, 0)
            attention_batches(e, batch)

        block = ctx.enter_context(nc.Block())

        @block.sync
        def _(e):
            def load_x(t, slot):
                e.dma_start(res[:, t, :, :], x[t].rearrange("(p j) d -> p j d", j=TILES)).then_inc(x_in[slot], 16)

            load_x(0, 0)
            e.dma_start(w1_raw[:, :], w1).then_inc(w_in, 16)
            e.dma_start(w2_raw[:, :].rearrange("p (f d) -> p f d", d=D), w2.rearrange("(f p) d -> p f d", p=P))\
                .then_inc(w_in, 16)
            load_x(1, 1)
            for to, of in ((b1_c, b1), (b2_r, b2), (wq_s, wq), (wk_s, wk), (wv_s, wv), (wo_s, wo),
                           (bq_c, bq), (bk_c, bk), (bv_r, bv), (bo_r, bo)):
                e.dma_start(to[:, :], of).then_inc(const_in, 16)
            with e.Fori(1, B // 2) as u:
                for slot in range(2):
                    e.wait_ge(x_in[slot], 16 * u)
                    load_x(2 * u + slot, slot)
            att_sync(e)

            def store(t):
                e.wait_ge(ffn[1].done, t + 1)
                e.dma_start(out[t].rearrange("(p j) d -> p j d", j=TILES), res[:, t, :, :]).then_inc(stored, 16)

            store(0)
            with e.Fori(1, B) as t:
                store(t)
            e.wait_ge(stored, 16 * B)

        @block.gpsimd
        def _(e):
            e.memset(ident[:, :], 0.0).then_inc(ident_set, 1)
            e.memset(minus_half[:, :], -0.5)
            e.memset(ones[:, :], 1.0).then_inc(ident_set, 1)
            e.wait_ge(ident_set, 1)
            e.affine_select(out=ident[:, :], in_=ident[:, :], compare_op=ALU.not_equal, fill=1.0,
                            base=0, pattern=[[-1, P]], channel_multiplier=1).then_inc(ident_set, 1)

            def fixed(n):
                if n == 0:
                    e.memset(q_rows[:, :, :, :].bitcast(F32), 0.0).then_inc(fixed_set, 1)
                elif n == 1:
                    e.memset(k_rows[:, :, :, :].bitcast(F32), 0.0).then_inc(fixed_set, 1)
                elif n == 2:
                    e.memset(v_aug[:, :, :, :, :], 0.0).then_inc(fixed_set, 1)
                else:
                    e.wait_ge(fixed_set, 3)
                    for slot in range(2):
                        e.memset(v_aug[:, slot, :, :, DH], 1.0).then_inc(fixed_set, 1)
                    e.wait_ge(fixed_set, 5)
                    e.wait_ge(ffn[0].rstd_ready, 6)
                    e.wait_ge(ffn[0].biased, 4)
                    for half in range(2):
                        e.memset(k_rows[64 * half + MROW:64 * half + MROW + 2, :, :, :].bitcast(F32), 1.0)\
                            .then_inc(fixed_set, 1)
                    e.wait_ge(fixed_set, 7)

            first = ffn_gpsimd(e, ffn[0])
            e.wait_ge(ident_set, 2)
            for t in range(2):
                ln_rstd(e, t, t, ffn[0])
            e.wait_ge(const_in, 160)
            e.wait_ge(w_ready, 3)
            for n in range(4):
                first(n, n % 2)
                fixed(n)
            with e.Fori(4, B - 4, 2) as t:
                first(t, 0)
                first(t + 1, 1)
            att_gpsimd(e)(first)
            second = ffn_gpsimd(e, ffn[1])
            for t in range(2):
                ln_rstd(e, t, t, ffn[1])
            for t in range(2):
                second(t, t)
            with e.Fori(2, B - 2, 2) as t:
                second(t, 0)
                second(t + 1, 1)
            for t in range(B - 2, B):
                second(t, t % 2)

        @block.scalar
        def _(e):
            e.wait_ge(w_in, 32)
            for n, raw in enumerate((w1_raw, w2_raw)):
                e.activation(w_abs[:, n, :], raw[:, :], ACT.Abs, accum_out=w_sum[:, n:n + 1]).then_inc(w_ready, 1)
            normalise(e, 0, 0, ffn[0], (ffn[0].t_ps, 0))
            e.wait_ge(const_in, 160)
            e.mul(bq_scaled[:, :], bq_c[:, :], SCALE)
            e.mul(b2_half[:, :], b2_r[:, :], 0.5).then_inc(w_ready, 1)
            step = ffn_scalar(e, ffn[0])
            step(0, 0)
            e.wait_ge(w_ready, 3)
            step(1, 1)
            ffn_middle(e, step)
            begin, end = att_scalar(e)
            begin(step)
            step = ffn_scalar(e, ffn[1])
            end(step, lambda: normalise(e, 0, 0, ffn[1], (ffn[1].t_ps, 0)))
            with e.Fori(4, B - 4, 2) as t:
                step(t, 0)
                step(t + 1, 1)
            ffn_end(e, step)

        @block.vector
        def _(e):
            def x_loaded(t, slot):
                if isinstance(t, int):
                    e.wait_ge(x_in[slot], 16 * (t // 2 + 1))
                else:
                    e.wait_ge(x_in[slot], 8 * (t - slot) + 16)

            step, first_norm = ffn_vector(e, ffn[0], x_loaded)
            first_norm(0)
            first_norm(1)
            e.wait_ge(sums_ps, 1)
            e.tensor_scalar(w_scale[:, :], bank[7][:, 0:2], 1.0 / (D * F), 1e-8, ALU.mult, ALU.max).then_inc(w_step, 1)
            e.wait_ge(w_step, 1)
            e.tensor_scalar(half_up[:, :], w_scale[:, :], 0.5, None, ALU.mult)
            e.tensor_scalar(half_down[:, :], w_scale[:, :], -0.5, None, ALU.mult).then_inc(w_step, 1)
            e.wait_ge(w_step, 2)
            for n, raw in enumerate((w1_raw, w2_raw)):
                i = e.tensor_scalar(w_abs[:, n, :], raw[:, :], half_down[:, n:n + 1], None, ALU.is_lt)
            i.then_inc(w_step, 1)
            e.wait_ge(w_step, 3)
            for n, (raw, to) in enumerate(((w1_raw, w1_t[:, :]), (w2_raw, w2_t[:, :, :].rearrange("p f d -> p (f d)")))):
                i = e.scalar_tensor_tensor(to, raw[:, :], half_up[:, n:n + 1], w_abs[:, n, :], ALU.is_gt, ALU.subtract)
            i.then_inc(w_step, 1)
            step(0, 0)
            step(1, 1)
            ffn_middle(e, step)
            begin, end = att_vector(e)
            begin(step)
            step, first_norm = ffn_vector(e, ffn[1], lambda t, slot: e.wait_ge(att_done, t + 1))
            end(step, first_norm)
            with e.Fori(4, B - 4, 2) as t:
                step(t, 0)
                step(t + 1, 1)
            ffn_end(e, step)

        @block.tensor
        def _(e):
            e.wait_ge(ident_set, 3)
            e.wait_ge(w_ready, 2)
            e.matmul(bank[7][:, 0:2], ones[:, :], w_sum[:, :], start=True, stop=True).then_inc(sums_ps, 1)
            step = ffn_tensor(e, ffn[0])
            step(0, 0)
            e.wait_ge(w_step, 4)
            step(1, 1)
            ffn_middle(e, step)
            begin, end = att_tensor(e)
            begin(step)
            step = ffn_tensor(e, ffn[1])
            end(step)
            with e.Fori(4, B - 4, 2) as t:
                step(t, 0)
                step(t + 1, 1)
            ffn_end(e, step)


def kernel(**inputs):
    import numpy as np
    import concourse.bacc as bacc
    from concourse.bass_utils import run_bass_kernel_spmd

    def rows(v):
        return np.broadcast_to(v, (P, v.shape[0]))

    def columns(v):
        return v.reshape(-1, P).T

    i = {k.removeprefix("L0_"): np.asarray(v) for k, v in inputs.items()}
    laid = {
        "x": i["attn_x"], "w1": i["ffn_W1"].T, "b1": columns(i["ffn_b1"]), "w2": i["ffn_W2"].T, "b2": rows(i["ffn_b2"]),
        "wq": i["attn_wq"].T, "wk": i["attn_wk"].T, "wv": i["attn_wv"].T, "wo": i["attn_wo"].T,
        "bq": columns(i["attn_bq"]), "bk": columns(i["attn_bk"]), "bv": rows(i["attn_bv"]), "bo": rows(i["attn_bo"]),
    }
    nc = bacc.Bacc("TRN2", target_bir_lowering=False, num_devices=1)
    arrays, args = {}, []
    for name, a in laid.items():
        a = np.ascontiguousarray(a)
        arrays[f"in_{name}"] = a
        args.append(nc.dram_tensor(f"in_{name}", a.shape, mybir.dt.from_np(a.dtype), kind="ExternalInput").ap())
    out = nc.dram_tensor("out", laid["x"].shape, F32, kind="ExternalOutput").ap()
    build(nc, *args, out)
    r = run_bass_kernel_spmd(nc, [arrays], core_ids=[0])
    return r.results[0]["out"]
```

```python
from contextlib import ExitStack

import concourse.bass as bass
from concourse import mybir

F32 = mybir.dt.float32
F32R = mybir.dt.float32r
ALU = mybir.AluOpType
ACT = mybir.ActivationFunctionType
AX = mybir.AxisListType

P = 128
EPS = 1e-5
HEADS = 16
GROUP = 4
HPG = GROUP // 2
BANK_OF = ((0, 1, 2, 1), (0, 2, 1, 2))
BANK_AGO = (4, 3, 3, 2)
ST_ORDER, S_ORDER = (0, 2, 1, 3), (1, 3, 0, 2)


def wait(engine, semaphore, value):
    if not isinstance(value, int) or value > 0:
        engine.wait_ge(semaphore, value)


def build(nc, x, w1, b1, w2, b2, wq, wk, wv, wo, bq, bk, bv, bo, out):
    B, L, D = x.shape
    F = w1.shape[1]
    TILES = L // P
    FT = F // P
    DH = D // HEADS
    NG = HEADS // GROUP
    STEPS = NG * TILES
    SCALE = 1.0 / HEADS ** 0.5
    VW = 32
    ROWS = 4 * DH
    MROW = ROWS

    with ExitStack() as ctx:
        def sb(name, shape, dt=F32):
            return ctx.enter_context(nc.sbuf_tensor(name, shape, dt))

        def sem(name):
            return ctx.enter_context(nc.semaphore(name))

        bank = [ctx.enter_context(nc.psum_tensor(f"bank{k}", [P, 512], F32)) for k in range(8)]
        s_bank, st_bank, o_bank, misc = bank[0:3], bank[3:6], bank[6], bank[7]
        f_t, f_h, f_o = bank[0], bank[1:5], bank[5]

        q_stack = nc.dram_tensor("q_stack", [B, HEADS, 4, DH, L], F32).ap()
        k_stack = nc.dram_tensor("k_stack", [B, HEADS, 4, DH, L], F32).ap()
        m_stack = nc.dram_tensor("m_stack", [B * NG, 2, 2 * HPG * TILES, P], F32).ap()

        res = sb("res", [P, B, TILES, D])
        w1_raw = sb("w1_raw", [P, F])
        w2_raw = sb("w2_raw", [P, F])
        w_abs = sb("w_abs", [P, 2, F])
        w_sum = sb("w_sum", [P, 2])
        w_scale = sb("w_scale", [P, 2])
        half_up, half_down = sb("half_up", [P, 2]), sb("half_down", [P, 2])
        w1_t = sb("w1_t", [P, F], F32R)
        w2_t = sb("w2_t", [P, FT, D])
        wq_s, wk_s, wv_s, wo_s = (sb(n, [P, D]) for n in ("wq_s", "wk_s", "wv_s", "wo_s"))
        b1_c = sb("b1_c", [P, FT])
        b2_r, b2_half, bv_r, bo_r = (sb(n, [P, D]) for n in ("b2_r", "b2_half", "bv_r", "bo_r"))
        bq_c, bq_scaled, bk_c = (sb(n, [P, 1]) for n in ("bq_c", "bq_scaled", "bk_c"))
        ones = sb("ones", [P, P])
        ident = sb("ident", [P, P])

        minus_half = sb("minus_half", [P, TILES])

        class Norm:

            def __init__(self, name, slots):
                self.slots = slots
                self.stats = sb(f"{name}_stats", [P, TILES, 6])
                self.mean_var = sb(f"{name}_mean_var", [P, slots, TILES, 2])
                self.var_eps = sb(f"{name}_var_eps", [P, slots, TILES])
                self.rstd = sb(f"{name}_rstd", [P, slots, TILES])
                self.xn = sb(f"{name}_xn", [P, slots, TILES, D])

        ffn_norm, att_norm = Norm("ffn", 2), Norm("att", 1)
        x_hi = sb("x_hi", [P, 2, L], F32R)
        x_lo = sb("x_lo", [P, 2, L], F32R)
        h = sb("h", [P, 2, FT, L])

        x_t = sb("x_t", [P, L])
        q_full = sb("q_full", [P, L])
        k_full = sb("k_full", [P, L])
        q_parts = sb("q_parts", [P, 2, L], F32R)
        k_parts = sb("k_parts", [P, 2, L], F32R)
        v_aug = sb("v_aug", [P, 2, TILES, HEADS, VW])
        q_rows = sb("q_rows", [P, NG, HPG, L], F32R)
        k_rows = sb("k_rows", [P, NG, HPG, L], F32R)
        row_max = sb("row_max", [P, 2, 2, HPG, TILES])
        m_parts = sb("m_parts", [2 * HPG * TILES, 2, 2, P], F32R)
        probs = sb("probs", [P, 2, GROUP, L])
        o_sb = sb("o_sb", [P, 2, L])
        inv_sum = sb("inv_sum", [P, 2, TILES, GROUP])
        attn = sb("attn", [P, TILES, D])
        attn_t = sb("attn_t", [P, L])

        x_in = [sem("x_in_even"), sem("x_in_odd")]
        w_in, const_in = sem("w_in"), sem("const_in")
        w_step, w_ready, sums_ps, ident_set = sem("w_step"), sem("w_ready"), sem("sums_ps"), sem("ident_set")
        fixed_set = sem("fixed_set")

        class Ffn:

            def __init__(self, n):
                self.norm = ffn_norm
                self.stat_step = sem(f"f{n}_stat_step")
                self.rstd_ready = sem(f"f{n}_rstd_ready")
                self.xn_ready = sem(f"f{n}_xn_ready")
                self.t_ps = sem(f"f{n}_t_ps")
                self.hi_ready = sem(f"f{n}_hi_ready")
                self.lo_ready = sem(f"f{n}_lo_ready")
                self.h_ps = sem(f"f{n}_h_ps")
                self.h_ready = sem(f"f{n}_h_ready")
                self.o_ps = sem(f"f{n}_o_ps")
                self.biased = sem(f"f{n}_biased")
                self.done = sem(f"f{n}_done")

        ffn = [Ffn(0), Ffn(1)]

        xt_ps, xt_ready = sem("xt_ps"), sem("xt_ready")
        q_ps, k_ps, v_ps = sem("q_ps"), sem("k_ps"), sem("v_ps")
        q_ready, k_ready, v_ready = sem("q_ready"), sem("k_ready"), sem("v_ready")
        qh_ready, kh_ready, ql_ready, kl_ready = sem("qh_ready"), sem("kh_ready"), sem("ql_ready"), sem("kl_ready")
        ones_in, stack_written = sem("ones_in"), sem("stack_written")
        rows_in = [sem(f"rows_in{c}") for c in range(NG)]
        s_ps, s_used = sem("s_ps"), sem("s_used")
        mt_ps, mh_ready, ml_ready = sem("mt_ps"), sem("mh_ready"), sem("ml_ready")
        m_written = sem("m_written")
        m_in = [sem(f"m_in{c}") for c in range(NG)]
        st_ps, exp_done, pv_done = sem("st_ps"), sem("exp_done"), sem("pv_done")
        o_ready, ot_ps, inv_ready, attn_ready = sem("o_ready"), sem("ot_ps"), sem("inv_ready"), sem("attn_ready")
        at_ps, at_ready, op_ps = sem("at_ps"), sem("at_ready"), sem("op_ps")
        att_biased, att_done = sem("att_biased"), sem("att_done")
        stored = sem("stored")

        class Att:

            norm = att_norm
            stat_step, rstd_ready = sem("stat_step"), sem("rstd_ready")
            xn_ready = sem("xn_ready")

        att = Att

        def ln_stats(e, t, before, s):
            before()
            for j in range(TILES):
                i = e.bn_stats(s.norm.stats[:, j, :], res[:, t, j, :])
            i.then_inc(s.stat_step, 1)

        def ln_stats_done(e, t, s):
            wait(e, s.xn_ready, t + 1 - s.norm.slots)
            e.wait_ge(s.stat_step, 3 * t + 1)

        def ln_aggregate(e, t, slot, s):
            if isinstance(t, int):
                ln_stats_done(e, t, s)
            for j in range(TILES):
                i = e.bn_aggr(s.norm.mean_var[:, slot, j, :], s.norm.stats[:, j, :])
            i.then_inc(s.stat_step, 1)

        def ln_add_eps(e, t, slot, s):
            e.wait_ge(s.stat_step, 3 * t + 2)
            e.tensor_scalar(s.norm.var_eps[:, slot, :], s.norm.mean_var[:, slot, :, 1], EPS, None, ALU.add)\
                .then_inc(s.stat_step, 1)

        def ln_rstd(e, t, slot, s):
            e.wait_ge(s.stat_step, 3 * t + 3)
            e.tensor_tensor(s.norm.rstd[:, slot, :], s.norm.var_eps[:, slot, :], minus_half[:, :], ALU.pow)\
                .then_inc(s.rstd_ready, 1)

        def normalise(e, t, slot, s, turned, tiles=range(TILES)):
            if tiles[0] == 0:
                wait(e, turned, t + 1 - s.norm.slots)
                e.wait_ge(s.rstd_ready, t + 1)
            for j in tiles:
                i = e.tensor_scalar(s.norm.xn[:, slot, j, :], res[:, t, j, :], s.norm.mean_var[:, slot, j, 0:1],
                                    s.norm.rstd[:, slot, j:j + 1], ALU.subtract, ALU.mult)
            if tiles[-1] == TILES - 1:
                i.then_inc(s.xn_ready, 1)

        def parts_of(t):
            if not isinstance(t, int):
                return True, True, True, True, True
            return t < B, 1 <= t <= B, t >= 2, t + 1 < B, t + 2 < B

        def ffn_middle(e, step, in_third=None):
            step(2, 0)
            if in_third:
                step(3, 1, None, in_third)
            else:
                step(3, 1)
            with e.Fori(4, B - 8, 2) as t:
                step(t, 0)
                step(t + 1, 1)

        def ffn_end(e, step):
            for t in range(B - 4, B + 2):
                step(t, t % 2)

        def ffn_tensor(e, s):
            def step(t, slot, before_unit=None, after_unit=None):
                transpose, hidden, output, _, _ = parts_of(t)
                if transpose:
                    e.wait_ge(s.xn_ready, t + 1)
                    wait(e, s.lo_ready, t)
                    for j in range(TILES):
                        i = e.transpose(f_t[:, j * P:(j + 1) * P], s.norm.xn[:, slot, j, :], ident[:, :])
                    i.then_inc(s.t_ps, 1)
                if hidden:
                    e.wait_ge(s.lo_ready, t)
                    for f in range(FT):
                        wait(e, s.h_ready, (t - 2) * FT + f + 1)
                        e.matmul(f_h[f][:, :], w1_t[:, f * P:(f + 1) * P], x_hi[:, 1 - slot, :],
                                 start=True, stop=False)
                        e.matmul(f_h[f][:, :], w1_t[:, f * P:(f + 1) * P], x_lo[:, 1 - slot, :],
                                 start=False, stop=True).then_inc(s.h_ps, 1)
                        if after_unit:
                            after_unit(f)
                if output:
                    e.wait_ge(s.h_ready, (t - 1) * FT)
                    wait(e, s.done, t - 2)
                    for j in range(TILES):
                        if before_unit:
                            before_unit(FT + j)
                        for f in range(FT):
                            i = e.matmul(f_o[:, j * D:(j + 1) * D], h[:, slot, f, j * P:(j + 1) * P],
                                         w2_t[:, f, :], start=(f == 0), stop=(f == FT - 1))
                        if j == TILES - 1:
                            i.then_inc(s.o_ps, 1)
                        if after_unit:
                            after_unit(FT + j)
            return step

        def ffn_scalar(e, s):
            def step(t, slot, between=None):
                transpose, hidden, _, _, _ = parts_of(t)
                if transpose:
                    e.wait_ge(s.t_ps, t + 1)
                    wait(e, s.h_ps, (t - 1) * FT)
                    e.activation(x_hi[:, slot, :], f_t[:, :], ACT.Copy).then_inc(s.hi_ready, 1)
                if between:
                    between()
                if hidden:
                    wait(e, s.o_ps, t - 2)
                    for f in range(FT):
                        e.wait_ge(s.h_ps, (t - 1) * FT + f + 1)
                        e.activation(h[:, 1 - slot, f, :], f_h[f][:, :], ACT.Gelu, bias=b1_c[:, f:f + 1])\
                            .then_inc(s.h_ready, 1)
            return step

        def ffn_vector(e, s, before):
            def first_stats(t):
                ln_stats(e, t, lambda: before(t, t), s)
                ln_aggregate(e, t, t, s)
                ln_add_eps(e, t, t, s)

            def low(t, slot):
                e.wait_ge(s.hi_ready, t + 1)
                wait(e, s.h_ps, (t - 1) * FT)
                e.tensor_tensor(x_lo[:, slot, :], f_t[:, :], x_hi[:, slot, :], ALU.subtract)\
                    .then_inc(s.lo_ready, 1)

            def step(t, slot, after_low=None, before_output=None, low_first=False):
                transpose, _, output, norm, stats = parts_of(t)
                if low_first:
                    low(t, slot)
                if norm:
                    normalise(e, t + 1, 1 - slot, s, s.t_ps)
                if stats:
                    ln_stats(e, t + 2, lambda: before(t + 2, slot), s)
                    if not isinstance(t, int):
                        ln_stats_done(e, t + 2, s)
                if transpose and not low_first:
                    low(t, slot)
                    if after_low:
                        after_low()
                if stats:
                    ln_aggregate(e, t + 2, slot, s)
                    ln_add_eps(e, t + 2, slot, s)
                if before_output:
                    before_output()
                if output:
                    e.wait_ge(s.o_ps, t - 1)
                    e.wait_ge(s.biased, t - 1)
                    r = res[:, t - 2, :, :].rearrange("p j d -> p (j d)")
                    e.scalar_tensor_tensor(r, f_o[:, :], 0.5, r, ALU.mult, ALU.add).then_inc(s.done, 1)
            return step, first_stats

        def add_row(e, t, row, xn_done, signal):
            e.wait_ge(xn_done, t + 1)
            e.tensor_tensor(res[:, t, :, :], res[:, t, :, :],
                            row[:, :].unsqueeze(1).broadcast_to([P, TILES, D]), ALU.add).then_inc(signal, 1)

        def ffn_gpsimd(e, s):
            def step(t, slot):
                if parts_of(t)[-1]:
                    ln_rstd(e, t + 2, slot, s)
                add_row(e, t, b2_half, s.xn_ready, s.biased)
            return step

        V_STEP, AT_STEP, OP_STEP, X_STEP, Q_STEP, K_STEP = 2, 3, 6, 10, 11, 14

        def attention_batches(e, batch, in_last=None):
            batch(0, 0)
            with e.Fori(1, B - 3, 2) as b:
                batch(b, 1)
                batch(b + 1, 0)
            for b in range(B - 3, B - 1):
                batch(b, b % 2)
            if in_last:
                batch(B - 1, (B - 1) % 2, in_last)
            else:
                batch(B - 1, (B - 1) % 2)

        def neighbours(b):
            if not isinstance(b, int):
                return True, True, True
            return b > 0, b + 1 < B, b + 2 < B

        EARLY_AT = {B - 4: (3, 5, 7), B - 3: (1, 4, 5, 7), B - 2: (1, 4, 5, 7), B - 1: (1, 3, 4, 6, 7)}
        EARLY_FIRST = {B - 4: 0, B - 3: 3, B - 2: 7, B - 1: 11, B: 16, B + 1: 24}

        def shifted_bank(kt, i, ahead):
            return st_bank[BANK_OF[kt % 2][i]] if ahead else bank[(3, 4, 5, 2)[i]]

        def early_bank(n):
            return o_bank if n < 16 or n % 2 else f_t

        def att_tensor(e):
            def half(i):
                return 64 * (i % 2), i // 2

            def transposed_x(b):
                e.wait_ge(att.xn_ready, b + 1)
                for j in range(TILES):
                    m = e.transpose(misc[:, j * P:(j + 1) * P], att_norm.xn[:, 0, j, :], ident[:, :])
                m.then_inc(xt_ps, 1)

            def project_q(b):
                e.wait_ge(xt_ready, b + 1)
                e.matmul(misc[:, :], wq_s[:, :], x_t[:, :], start=True, stop=True).then_inc(q_ps, 1)

            def project_k(b):
                e.matmul(misc[:, :], wk_s[:, :], x_t[:, :], start=True, stop=True).then_inc(k_ps, 1)

            def project_v(b):
                for j in range(TILES):
                    m = e.matmul(misc[:, j * D:(j + 1) * D], x_t[:, j * P:(j + 1) * P], wv_s[:, :],
                                 start=True, stop=True)
                m.then_inc(v_ps, 1)

            def early_score(n):
                g, kt, i = n // 16, n // 4 % 4, n % 4
                if g == 0:
                    wait(e, s_used, n)
                elif n > 16:
                    e.wait_ge(s_used, n - 1)
                else:
                    e.wait_ge(ffn[0].lo_ready, B)
                p, hh = half(S_ORDER[i])
                e.matmul(early_bank(n)[:, :], q_rows[p:p + 64, g, hh, kt * P:(kt + 1) * P],
                         k_rows[p:p + 64, g, hh, :], start=True, stop=True).then_inc(s_ps, 1)

            def score(g, c, kt, i):
                n = 16 * g + 4 * kt + i
                if i > 0:
                    wait(e, s_used, n + 1 - BANK_AGO[i])
                p, hh = half(S_ORDER[i])
                e.matmul(s_bank[BANK_OF[kt % 2][i]][:, :], q_rows[p:p + 64, c, hh, kt * P:(kt + 1) * P],
                         k_rows[p:p + 64, c, hh, :], start=True, stop=True).then_inc(s_ps, 1)

            def shifted(g, c, kt, i, ahead):
                n = 16 * g + 4 * kt + i
                if not ahead:
                    ago = max(BANK_AGO[1:]) if (c, kt) == (NG - 2, 0) else GROUP
                    e.wait_ge(exp_done, n + 1 - ago)
                elif i in (1, 3):
                    wait(e, exp_done, n + 1 - BANK_AGO[i])
                p, hh = half(ST_ORDER[i])
                e.matmul(shifted_bank(kt, i, ahead)[:, :], k_rows[p:p + 64, c, hh, kt * P:(kt + 1) * P],
                         q_rows[p:p + 64, c, hh, :], start=True, stop=True).then_inc(st_ps, 1)

            def weighted(g, c, kt, vslot):
                if kt == 0:
                    wait(e, o_ready, g)
                e.wait_ge(exp_done, 16 * g + 4 * kt + 4)
                for i in range(GROUP):
                    m = e.matmul(o_bank[VW * i:VW * i + VW, :], v_aug[:, vslot, kt, GROUP * c + i, :],
                                 probs[:, kt % 2, i, :], start=(kt == 0), stop=(kt == TILES - 1))
                m.then_inc(pv_done, 1)

            def transposed_max(g, slot):
                e.wait_ge(s_used, 16 * g + 16)
                e.transpose(misc[0:4 * TILES, 0:P],
                            row_max[:, slot, :, :, :].rearrange("p a b j -> p (a b j)"), ident[:, :])\
                    .then_inc(mt_ps, 1)

            def transposed_o(g, slot):
                e.wait_ge(o_ready, g + 1)
                for j in range(TILES):
                    m = e.transpose(misc[:, j * P:(j + 1) * P], o_sb[:, slot, j * P:(j + 1) * P], ident[:, :])
                m.then_inc(ot_ps, 1)

            def transposed_attn(b):
                e.wait_ge(attn_ready, NG * b + NG)
                for j in range(TILES):
                    m = e.transpose(misc[:, j * P:(j + 1) * P], attn[:, j, :], ident[:, :])
                m.then_inc(at_ps, 1)

            def project_out(b):
                e.wait_ge(at_ready, b + 1)
                for j in range(TILES):
                    m = e.matmul(misc[:, j * D:(j + 1) * D], attn_t[:, j * P:(j + 1) * P], wo_s[:, :],
                                 start=True, stop=True)
                m.then_inc(op_ps, 1)

            def small_work(b, s):
                before, after, after2 = neighbours(b)
                c, kt = s // TILES, s % TILES
                g = NG * b + c
                if kt == 0 and (c + 1 < NG or after):
                    if s == 0:
                        if after:
                            e.wait_ge(k_ready, b + 2)
                        else:
                            e.wait_ge(attn_ready, NG * b - 1)
                    elif s == 4:
                        if before:
                            e.wait_ge(at_ready, b)
                        else:
                            e.wait_ge(v_ready, b + 2)
                    elif s == 8:
                        if before:
                            e.wait_ge(att_done, b)
                        else:
                            e.wait_ge(attn_ready, NG * b + 1)
                    elif after2:
                        e.wait_ge(q_ready, b + 3)
                    else:
                        e.wait_ge(attn_ready, NG * b + 2)
                    e.wait_ge(ml_ready, g + 1)
                    transposed_max(g + 1, (c + 1) % 2)
                elif kt == 1 and (c > 0 or before):
                    if c + 1 < NG or after:
                        e.wait_ge(ml_ready, g + 2)
                    else:
                        e.wait_ge(attn_ready, g - 1)
                    transposed_o(g - 1, (c - 1) % 2)
                elif s == V_STEP and after:
                    if before:
                        e.wait_ge(attn_ready, NG * b)
                    else:
                        e.wait_ge(ml_ready, g + 2)
                    project_v(b + 1)
                elif s == AT_STEP and before:
                    if after:
                        e.wait_ge(v_ready, b + 2)
                    transposed_attn(b - 1)
                elif s == OP_STEP and before:
                    e.wait_ge(attn_ready, NG * b + 1)
                    project_out(b - 1)
                elif s == X_STEP and after2:
                    e.wait_ge(attn_ready, NG * b + 2)
                    transposed_x(b + 2)
                elif s == Q_STEP and after2:
                    project_q(b + 2)
                elif s == K_STEP and after2:
                    e.wait_ge(attn_ready, NG * b + 3)
                    project_k(b + 2)

            def batch(b, slot, in_last=None):
                before, after, _ = neighbours(b)
                for s in range(STEPS):
                    c, kt = s // TILES, s % TILES
                    g = NG * b + c
                    ahead = c + 2 < NG or after
                    cs = (c + 2) % NG
                    if kt == 0:
                        e.wait_ge(m_in[c], 32 * (b + 1))
                        if ahead:
                            e.wait_ge(rows_in[cs], 96 * (b + 1 + (c + 2) // NG))
                    for i in range(GROUP):
                        if not before and s == 0 and i == 2:
                            e.wait_ge(ffn[0].done, B)
                        if not ahead and s == STEPS - 2 * TILES and i == 3:
                            e.wait_ge(s_used, 16 * NG * B)
                        shifted(g, c, kt, i, ahead)
                        if not before and s == 0 and i == 0:
                            e.wait_ge(s_used, 2 * 16 - 1)
                        if ahead:
                            score(g + 2, cs, kt, i)
                        if i == (1 if ahead else 2):
                            if s > 0:
                                weighted(NG * b + (s - 1) // TILES, (s - 1) // TILES, (s - 1) % TILES, slot)
                            elif before:
                                weighted(g - 1, NG - 1, TILES - 1, 1 - slot)
                    small_work(b, s)
                    if in_last:
                        in_last(s)

            def begin(step, next_step):
                def next_phase(s):
                    if s == 13:
                        next_step(0, 0)

                def last_units(u):
                    if u == 0:
                        e.wait_ge(rows_in[1], 96)
                    early_score(16 + u)
                    if u == 0:
                        e.wait_ge(k_ready, 2)
                        transposed_max(0, 0)

                def two_before(u):
                    early_score(16 + 2 * u)
                    early_score(17 + 2 * u)

                for t in range(B - 8, B):
                    def after_unit(u):
                        if u == 2:
                            if t == B - 8:
                                transposed_x(0)
                            elif t == B - 7:
                                e.wait_ge(q_ready, 1)
                                project_k(0)
                            elif t == B - 3:
                                e.wait_ge(v_ready, 1)
                                transposed_x(1)
                            elif t == B - 2:
                                e.wait_ge(q_ready, 2)
                                project_k(1)
                        elif u == 7:
                            if t == B - 8:
                                project_q(0)
                            elif t == B - 7:
                                e.wait_ge(k_ready, 1)
                                project_v(0)
                            elif t == B - 3:
                                project_q(1)
                        if t in EARLY_AT and u in EARLY_AT[t]:
                            if t == B - 4 and u == EARLY_AT[t][0]:
                                e.wait_ge(rows_in[0], 96)
                            early_score(EARLY_FIRST[t] + EARLY_AT[t].index(u))
                    step(t, t % 2, None, after_unit)
                step(B, 0, None, last_units)
                step(B + 1, 1, two_before)
                attention_batches(e, batch, next_phase)

            last = NG * B - 1

            def end(step):
                def banks_read(u):
                    if u == 0:
                        e.wait_ge(exp_done, 16 * last + 16)

                def attention_turned(u):
                    if u == 3:
                        transposed_attn(B - 1)

                step(1, 1, None, banks_read)
                weighted(last, NG - 1, TILES - 1, 1)
                step(2, 0)
                e.wait_ge(attn_ready, last)
                transposed_o(last, 1)
                step(3, 1, None, attention_turned)
                project_out(B - 1)
            return begin, end

        def att_scalar(e):
            def x_transposed(b):
                e.wait_ge(xt_ps, b + 1)
                wait(e, v_ps, b)
                e.activation(x_t[:, :], misc[:, :], ACT.Copy).then_inc(xt_ready, 1)

            def q_out(b):
                e.wait_ge(q_ps, b + 1)
                wait(e, ql_ready, b)
                e.activation(q_full[:, :], misc[:, :], ACT.Identity, bias=bq_scaled[:, :], scale=SCALE)\
                    .then_inc(q_ready, 1)

            def k_out(b):
                e.wait_ge(k_ps, b + 1)
                wait(e, kl_ready, b)
                e.activation(k_full[:, :], misc[:, :], ACT.Identity, bias=bk_c[:, :]).then_inc(k_ready, 1)

            def max_high(g, slot):
                e.wait_ge(mt_ps, g + 1)
                wait(e, m_written, 16 * (g - 1))
                e.activation(m_parts[:, slot, 0, :], misc[0:4 * TILES, 0:P], ACT.Copy, scale=-1.0)\
                    .then_inc(mh_ready, 1)

            def o_out(g, slot):
                e.wait_ge(pv_done, TILES * (g + 1))
                wait(e, ot_ps, g - 1)
                e.activation(o_sb[:, slot, :], o_bank[:, :], ACT.Copy).then_inc(o_ready, 1)

            def attn_out(b):
                e.wait_ge(at_ps, b + 1)
                wait(e, op_ps, b)
                e.activation(attn_t[:, :], misc[:, :], ACT.Copy).then_inc(at_ready, 1)

            def batch(b, slot, in_last=None):
                before, after, after2 = neighbours(b)
                for s in range(STEPS):
                    c, kt = s // TILES, s % TILES
                    g = NG * b + c
                    ahead = c + 2 < NG or after
                    wait(e, pv_done, STEPS * b + s - 1)
                    for i in range(GROUP):
                        n = 16 * g + 4 * kt + i
                        e.wait_ge(st_ps, n + 1)
                        e.activation(probs[:, kt % 2, ST_ORDER[i], :], shifted_bank(kt, i, ahead)[:, :], ACT.Exp)\
                            .then_inc(exp_done, 1)
                        if in_last and i == 1:
                            in_last(s)
                        if kt == 0 and i == 2 and (c > 0 or before):
                            o_out(g - 1, (c - 1) % 2)
                    if kt == 0 and (c + 1 < NG or after):
                        max_high(g + 1, (c + 1) % 2)
                    if s == AT_STEP and before:
                        attn_out(b - 1)
                    if after2:
                        if s == X_STEP:
                            x_transposed(b + 2)
                        elif s == Q_STEP:
                            q_out(b + 2)
                        elif s == K_STEP:
                            k_out(b + 2)

            def begin(step, next_step):
                def next_phase(s):
                    if s == 14:
                        next_step(0, 0)

                for t in range(B - 8, B + 1):
                    def between():
                        if t == B - 7:
                            q_out(0)
                        elif t == B - 2:
                            q_out(1)
                        elif t == B:
                            max_high(0, 0)
                    step(t, t % 2, between)
                    if t == B - 8:
                        x_transposed(0)
                    elif t == B - 7:
                        k_out(0)
                    elif t == B - 3:
                        x_transposed(1)
                    elif t == B - 2:
                        k_out(1)
                attention_batches(e, batch, next_phase)

            def end(step):
                step(1, 1)
                o_out(NG * B - 1, 1)
                step(2, 0)
                step(3, 1)
                attn_out(B - 1)
            return begin, end

        def att_vector(e):
            def split(full, parts, source, signal, b):
                e.wait_ge(source, b + 1)
                wait(e, stack_written, 128 * b)
                e.tensor_copy(parts[:, 0, :], full[:, :]).then_inc(signal, 1)

            def v_out(b, slot):
                e.wait_ge(v_ps, b + 1)
                wait(e, pv_done, STEPS * (b - 1))
                e.tensor_tensor(v_aug[:, slot, :, :, 0:DH],
                                misc[:, :].rearrange("p (j h d) -> p j h d", j=TILES, d=DH),
                                bv_r[:, :].rearrange("p (h d) -> p h d", d=DH).unsqueeze(1)
                                .broadcast_to([P, TILES, HEADS, DH]), ALU.add).then_inc(v_ready, 1)

            def reduce_scores(g, c, kt, i, slot, source=None):
                n = 16 * g + 4 * kt + i
                source = source or s_bank[BANK_OF[kt % 2][i]]
                if kt == 0 and i == 0:
                    wait(e, mt_ps, g - 1)
                e.wait_ge(s_ps, n + 1)
                head = S_ORDER[i]
                e.tensor_reduce(row_max[:, slot, head % 2, head // 2, kt:kt + 1], source[:, :],
                                AX.X, ALU.max).then_inc(s_used, 1)

            def max_low(g, slot):
                e.wait_ge(mh_ready, g + 1)
                e.scalar_tensor_tensor(m_parts[:, slot, 1, :], misc[0:4 * TILES, 0:P], -1.0,
                                       m_parts[:, slot, 0, :], ALU.mult, ALU.subtract).then_inc(ml_ready, 1)

            o_view = misc[:, :].rearrange("p (j i r) -> p j i r", j=TILES, r=VW)

            def o_sums(g, slot):
                e.wait_ge(ot_ps, g + 1)
                e.reciprocal(inv_sum[:, slot, :, :], o_view[:, :, :, DH]).then_inc(inv_ready, 1)

            def o_scaled(b, g, c, slot):
                if c == 0:
                    wait(e, at_ps, b)
                e.wait_ge(inv_ready, g + 1)
                e.tensor_tensor(attn[:, :, GROUP * DH * c:GROUP * DH * (c + 1)].rearrange("p j (i d) -> p j i d", d=DH),
                                o_view[:, :, :, 0:DH],
                                inv_sum[:, slot, :, :].unsqueeze(3).broadcast_to([P, TILES, GROUP, DH]),
                                ALU.mult).then_inc(attn_ready, 1)

            def residual(b):
                e.wait_ge(op_ps, b + 1)
                e.wait_ge(att_biased, b + 1)
                r = res[:, b, :, :].rearrange("p j d -> p (j d)")
                e.tensor_tensor(r, misc[:, :], r, ALU.add).then_inc(att_done, 1)

            def batch(b, slot, in_last=None):
                before, after, after2 = neighbours(b)
                for s in range(STEPS):
                    c, kt = s // TILES, s % TILES
                    g = NG * b + c
                    ahead = c + 2 < NG or after
                    cs = (c + 2) % NG
                    if in_last:
                        in_last(s)
                    for i in range(GROUP):
                        if s == 6 and i == 1 and after2 and not isinstance(b, int):
                            ln_stats_done(e, b + 2, att)
                        if ahead:
                            reduce_scores(g + 2, cs, kt, i, c % 2)
                        if kt == 1 and i == 0 and (c + 1 < NG or after):
                            max_low(g + 1, (c + 1) % 2)
                        if kt == 1 and i == 3 and (c > 0 or before):
                            o_sums(g - 1, (c - 1) % 2)
                        if kt == 2 and i == 0 and (c > 0 or before):
                            o_scaled(b, g - 1, (c - 1) % NG, (c - 1) % 2)
                        if s == V_STEP + 1 and i == 0 and after:
                            v_out(b + 1, 1 - slot)
                        if s == OP_STEP + 1 and i == 0 and before:
                            residual(b - 1)
                        if after2:
                            if s == 5 and i == 1:
                                ln_stats(e, b + 2, lambda: e.wait_ge(ffn[0].done, b + 3), att)
                            elif s == 6 and i == 1:
                                ln_aggregate(e, b + 2, 0, att)
                            elif s == 6 and i == 3:
                                ln_add_eps(e, b + 2, 0, att)
                            elif s in (8, 9) and i % 2 == 0:
                                j = 2 * (s - 8) + i // 2
                                normalise(e, b + 2, 0, att, xt_ps, range(j, j + 1))
                            elif s == Q_STEP + 1 and i == 0:
                                split(q_full, q_parts, q_ready, qh_ready, b + 2)
                            elif s == K_STEP + 1 and i == 0:
                                split(k_full, k_parts, k_ready, kh_ready, b + 2)

            def stats(b):
                ln_stats(e, b, lambda: e.wait_ge(ffn[0].done, b + 1), att)
                ln_aggregate(e, b, 0, att)
                ln_add_eps(e, b, 0, att)

            def reduce_early(first, last):
                for n in range(first, last):
                    reduce_scores(n // 16, n // 16, n // 4 % 4, n % 4, n // 16, early_bank(n))

            def begin(step, next_step, next_stats):
                normalise(e, 0, 0, att, xt_ps)

                def next_phase(s):
                    if s in (8, 9):
                        next_stats(s - 8)
                    elif s == 10:
                        normalise(e, 0, 0, ffn[1], ffn[1].t_ps)
                    elif s == STEPS - 1:
                        next_step(0, 0)

                for t in range(B - 8, B + 2):
                    n = EARLY_FIRST.get(t)
                    last = n + len(EARLY_AT[t]) - 1 if t in EARLY_AT else None

                    def before_output():
                        if t == B - 8:
                            stats(1)
                        elif t == B - 7:
                            split(q_full, q_parts, q_ready, qh_ready, 0)
                        elif t == B - 6:
                            e.wait_ge(fixed_set, 6)
                            v_out(0, 0)
                        elif B - 4 <= t < B:
                            reduce_early(n + 1, n + 2)
                            if t == B - 2:
                                split(q_full, q_parts, q_ready, qh_ready, 1)
                            elif t == B - 1:
                                split(k_full, k_parts, k_ready, kh_ready, 1)
                            reduce_early(n + 2, last)
                        elif t == B:
                            reduce_early(n, n + 2)
                            max_low(0, 0)
                            reduce_early(n + 2, n + 7)
                        elif t == B + 1:
                            reduce_early(n, n + 8)
                    step(t, t % 2, lambda: reduce_early(n, n + 1) if last else None, before_output)
                    if t == B - 6:
                        normalise(e, 1, 0, att, xt_ps)
                    elif t == B - 7:
                        split(k_full, k_parts, k_ready, kh_ready, 0)
                    elif B - 4 <= t < B:
                        reduce_early(last, last + 1)
                    elif t == B:
                        reduce_early(n + 7, n + 8)
                attention_batches(e, batch, next_phase)

            def end(step):
                step(1, 1)
                step(2, 0)
                o_sums(NG * B - 1, 1)
                o_scaled(B, NG * B - 1, NG - 1, 1)
                step(3, 1)
                residual(B - 1)
            return begin, end, stats

        def att_gpsimd(e):
            def low(full, parts, high_ready, signal, b):
                e.wait_ge(high_ready, b + 1)
                e.tensor_tensor(parts[:, 1, :], full[:, :], parts[:, 0, :], ALU.subtract).then_inc(signal, 1)

            def batch(b):
                low(q_full, q_parts, qh_ready, ql_ready, b)
                low(k_full, k_parts, kh_ready, kl_ready, b)
                add_row(e, b, bo_r, att.xn_ready, att_biased)

            def begin(step):
                for t in range(B - 8, B):
                    step(t, t % 2)
                    if t == B - 8:
                        ln_rstd(e, 1, 0, att)
                    elif t == B - 7:
                        low(q_full, q_parts, qh_ready, ql_ready, 0)
                        low(k_full, k_parts, kh_ready, kl_ready, 0)
                    elif t == B - 5:
                        add_row(e, 0, bo_r, att.xn_ready, att_biased)
                batch(1)
                ln_rstd(e, 2, 0, att)
                with e.Fori(2, B - 1) as b:
                    batch(b)
                    ln_rstd(e, b + 1, 0, att)
                batch(B - 1)
            return begin

        def att_sync(e):
            def store_parts(b):
                for ready, parts, stack, order in ((ql_ready, q_parts, q_stack, (0, 1, 0, 1)),
                                                   (kl_ready, k_parts, k_stack, (0, 1, 1, 0))):
                    e.wait_ge(ready, b + 1)
                    for r, part in enumerate(order):
                        e.dma_start(stack[b, :, r, :, :], parts[:, part, :].bitcast(F32)).then_inc(stack_written, 16)

            def load_rows(b, c):
                wait(e, st_ps, 16 * (NG * b + c - NG + 1))
                for half in range(2):
                    e.dma_start(q_rows[64 * half + MROW:64 * half + MROW + 2, c, :, :].bitcast(F32),
                                q_rows[64 * half + MROW + 2:64 * half + MROW + 4, c, :, :].bitcast(F32))\
                        .then_inc(rows_in[c], 16)
                if c == 0:
                    e.wait_ge(stack_written, 128 * (b + 1))
                for half in range(2):
                    for rows, stack in ((q_rows, q_stack), (k_rows, k_stack)):
                        heads = stack[b, GROUP * c + half:GROUP * (c + 1):2, :, :, :]
                        e.dma_start(rows[64 * half:64 * half + ROWS, c, :, :].bitcast(F32),
                                    heads.rearrange("a r d n -> (r d) a n")).then_inc(rows_in[c], 16)

            def load_max(b, c, slot):
                g = NG * b + c
                e.wait_ge(ml_ready, g + 1)
                e.dma_start(m_stack[g].rearrange("t r p -> r t p"), m_parts[:, slot, :, :].bitcast(F32))\
                    .then_inc(m_written, 16)
                e.wait_ge(m_written, 16 * (g + 1))
                for half in range(2):
                    e.dma_start(q_rows[64 * half + MROW:64 * half + MROW + 2, c, :, :].bitcast(F32),
                                m_stack[g, :, HPG * TILES * half:HPG * TILES * (half + 1), :]
                                .rearrange("t (a j) p -> t a (j p)", a=HPG)).then_inc(m_in[c], 16)

            def batch(b, slot):
                _, after, after2 = neighbours(b)
                for c in range(NG):
                    if c + 3 < NG or after:
                        load_rows(b + (c + 3) // NG, (c + 3) % NG)
                    if c + 1 < NG or after:
                        load_max(b + (c + 1) // NG, (c + 1) % NG, (c + 1) % 2)
                if after2:
                    store_parts(b + 2)

            e.wait_ge(fixed_set, 2)
            e.wait_ge(ident_set, 2)
            for half in range(2):
                e.dma_start(k_rows[64 * half + MROW:64 * half + MROW + 2, :, :, :].bitcast(F32)
                            .rearrange("r c a (s d) -> r (c a s) d", d=P),
                            ones[0:2, :].unsqueeze(1).broadcast_to([2, NG * HPG * L // P, P])).then_inc(ones_in, 16)
            store_parts(0)
            e.wait_ge(ones_in, 32)
            for c in range(3):
                load_rows(0, c)
            store_parts(1)
            load_max(0, 0, 0)
            attention_batches(e, batch)

        block = ctx.enter_context(nc.Block())

        @block.sync
        def _(e):
            def load_x(t, slot):
                e.dma_start(res[:, t, :, :], x[t].rearrange("(p j) d -> p j d", j=TILES)).then_inc(x_in[slot], 16)

            load_x(0, 0)
            e.dma_start(w1_raw[:, :], w1).then_inc(w_in, 16)
            e.dma_start(w2_raw[:, :].rearrange("p (f d) -> p f d", d=D), w2.rearrange("(f p) d -> p f d", p=P))\
                .then_inc(w_in, 16)
            load_x(1, 1)
            for to, of in ((b1_c, b1), (b2_r, b2), (wq_s, wq), (wk_s, wk), (wv_s, wv), (wo_s, wo),
                           (bq_c, bq), (bk_c, bk), (bv_r, bv), (bo_r, bo)):
                e.dma_start(to[:, :], of).then_inc(const_in, 16)
            with e.Fori(1, B // 2) as u:
                for slot in range(2):
                    e.wait_ge(x_in[slot], 16 * u)
                    load_x(2 * u + slot, slot)
            att_sync(e)

            def store(t):
                e.wait_ge(ffn[1].done, t + 1)
                e.dma_start(out[t].rearrange("(p j) d -> p j d", j=TILES), res[:, t, :, :]).then_inc(stored, 16)

            store(0)
            with e.Fori(1, B) as t:
                store(t)
            e.wait_ge(stored, 16 * B)

        @block.gpsimd
        def _(e):
            e.memset(ident[:, :], 0.0).then_inc(ident_set, 1)
            e.memset(minus_half[:, :], -0.5)
            e.memset(ones[:, :], 1.0).then_inc(ident_set, 1)
            e.wait_ge(ident_set, 1)
            e.affine_select(out=ident[:, :], in_=ident[:, :], compare_op=ALU.not_equal, fill=1.0,
                            base=0, pattern=[[-1, P]], channel_multiplier=1).then_inc(ident_set, 1)

            def fixed(n):
                if n < 2:
                    e.memset(v_aug[:, n, :, :, :], 0.0).then_inc(fixed_set, 1)
                elif n == 2:
                    e.wait_ge(fixed_set, 4)
                    for slot in range(2):
                        e.memset(v_aug[:, slot, :, :, DH], 1.0).then_inc(fixed_set, 1)

            first = ffn_gpsimd(e, ffn[0])
            e.wait_ge(ident_set, 2)
            e.memset(q_rows[:, :, :, :].bitcast(F32), 0.0).then_inc(fixed_set, 1)
            for t in range(2):
                ln_rstd(e, t, t, ffn[0])
            e.memset(k_rows[:, :, :, :].bitcast(F32), 0.0).then_inc(fixed_set, 1)
            e.wait_ge(const_in, 160)
            e.wait_ge(w_ready, 3)
            for n in range(4):
                first(n, n % 2)
                fixed(n)
            ln_rstd(e, 0, 0, att)
            with e.Fori(4, B - 8, 2) as t:
                first(t, 0)
                first(t + 1, 1)
            att_gpsimd(e)(first)
            second = ffn_gpsimd(e, ffn[1])
            for t in range(2):
                ln_rstd(e, t, t, ffn[1])
            for t in range(2):
                second(t, t)
            with e.Fori(2, B - 2, 2) as t:
                second(t, 0)
                second(t + 1, 1)
            for t in range(B - 2, B):
                second(t, t % 2)

        @block.scalar
        def _(e):
            e.wait_ge(w_in, 32)
            for n, raw in enumerate((w1_raw, w2_raw)):
                e.activation(w_abs[:, n, :], raw[:, :], ACT.Abs, accum_out=w_sum[:, n:n + 1]).then_inc(w_ready, 1)
            e.wait_ge(const_in, 160)
            e.mul(bq_scaled[:, :], bq_c[:, :], SCALE)
            e.mul(b2_half[:, :], b2_r[:, :], 0.5).then_inc(w_ready, 1)
            step = ffn_scalar(e, ffn[0])
            step(0, 0)
            e.wait_ge(w_ready, 3)
            step(1, 1)
            ffn_middle(e, step)
            begin, end = att_scalar(e)
            first, step = step, ffn_scalar(e, ffn[1])
            begin(first, step)
            end(step)
            with e.Fori(4, B - 4, 2) as t:
                step(t, 0)
                step(t + 1, 1)
            ffn_end(e, step)

        @block.vector
        def _(e):
            def x_loaded(t, slot):
                if isinstance(t, int):
                    e.wait_ge(x_in[slot], 16 * (t // 2 + 1))
                else:
                    e.wait_ge(x_in[slot], 8 * (t - slot) + 16)

            step, first_stats = ffn_vector(e, ffn[0], x_loaded)
            first_stats(0)
            ln_stats(e, 1, lambda: x_loaded(1, 1), ffn[0])
            normalise(e, 0, 0, ffn[0], ffn[0].t_ps)
            ln_aggregate(e, 1, 1, ffn[0])
            ln_add_eps(e, 1, 1, ffn[0])
            e.wait_ge(sums_ps, 1)
            e.tensor_scalar(w_scale[:, :], bank[7][:, 0:2], 1.0 / (D * F), 1e-8, ALU.mult, ALU.max).then_inc(w_step, 1)
            e.wait_ge(w_step, 1)
            e.tensor_scalar(half_up[:, :], w_scale[:, :], 0.5, None, ALU.mult)
            e.tensor_scalar(half_down[:, :], w_scale[:, :], -0.5, None, ALU.mult).then_inc(w_step, 1)
            e.wait_ge(w_step, 2)

            def ternary(n, raw, to):
                e.tensor_scalar(w_abs[:, n, :], raw[:, :], half_down[:, n:n + 1], None, ALU.is_lt).then_inc(w_step, 1)
                e.wait_ge(w_step, 3 + 2 * n)
                e.scalar_tensor_tensor(to, raw[:, :], half_up[:, n:n + 1], w_abs[:, n, :], ALU.is_gt, ALU.subtract)\
                    .then_inc(w_step, 1)

            ternary(0, w1_raw, w1_t[:, :])
            step(0, 0, None, lambda: ternary(1, w2_raw, w2_t[:, :, :].rearrange("p f d -> p (f d)")), True)
            step(1, 1, None, None, True)
            begin, end, att_stats = att_vector(e)
            ffn_middle(e, step, lambda: att_stats(0))
            first = step
            step, first_stats = ffn_vector(e, ffn[1], lambda t, slot: e.wait_ge(att_done, t + 1))
            begin(first, step, first_stats)
            end(step)
            with e.Fori(4, B - 4, 2) as t:
                step(t, 0)
                step(t + 1, 1)
            ffn_end(e, step)

        @block.tensor
        def _(e):
            e.wait_ge(ident_set, 3)
            e.wait_ge(w_ready, 2)
            e.matmul(bank[7][:, 0:2], ones[:, :], w_sum[:, :], start=True, stop=True).then_inc(sums_ps, 1)
            step = ffn_tensor(e, ffn[0])
            step(0, 0)
            e.wait_ge(w_step, 4)
            step(1, 1)
            e.wait_ge(w_step, 6)
            ffn_middle(e, step)
            begin, end = att_tensor(e)
            first, step = step, ffn_tensor(e, ffn[1])
            begin(first, step)
            end(step)
            with e.Fori(4, B - 4, 2) as t:
                step(t, 0)
                step(t + 1, 1)
            ffn_end(e, step)


def kernel(**inputs):
    import numpy as np
    import concourse.bacc as bacc
    from concourse.bass_utils import run_bass_kernel_spmd

    def rows(v):
        return np.broadcast_to(v, (P, v.shape[0]))

    def columns(v):
        return v.reshape(-1, P).T

    i = {k.removeprefix("L0_"): np.asarray(v) for k, v in inputs.items()}
    laid = {
        "x": i["attn_x"], "w1": i["ffn_W1"].T, "b1": columns(i["ffn_b1"]), "w2": i["ffn_W2"].T, "b2": rows(i["ffn_b2"]),
        "wq": i["attn_wq"].T, "wk": i["attn_wk"].T, "wv": i["attn_wv"].T, "wo": i["attn_wo"].T,
        "bq": columns(i["attn_bq"]), "bk": columns(i["attn_bk"]), "bv": rows(i["attn_bv"]), "bo": rows(i["attn_bo"]),
    }
    nc = bacc.Bacc("TRN2", target_bir_lowering=False, num_devices=1)
    arrays, args = {}, []
    for name, a in laid.items():
        a = np.ascontiguousarray(a)
        arrays[f"in_{name}"] = a
        args.append(nc.dram_tensor(f"in_{name}", a.shape, mybir.dt.from_np(a.dtype), kind="ExternalInput").ap())
    out = nc.dram_tensor("out", laid["x"].shape, F32, kind="ExternalOutput").ap()
    build(nc, *args, out)
    r = run_bass_kernel_spmd(nc, [arrays], core_ids=[0])
    return r.results[0]["out"]
```
